# Optimizing a Trainium2 kernel written in Bass

```python
import numpy as np
import jax
import jax.numpy as jnp

def _softmax(x, axis=-1):
    return jax.nn.softmax(x, axis=axis)

def _gelu(x):
    return jax.nn.gelu(x, approximate=True)

def _silu(x):
    return jax.nn.silu(x)

def _sigmoid(x):
    return jax.nn.sigmoid(x)

def _layernorm(x, axis=-1, eps=1e-05):
    m = jnp.mean(x, axis=axis, keepdims=True)
    v = jnp.var(x, axis=axis, keepdims=True)
    return (x - m) / jnp.sqrt(v + eps)

def _scatter_add(tgt, idx, src, axis=0):
    return tgt.at[idx].add(src)

def _segment_sum(src, seg, n):
    return jax.ops.segment_sum(src, seg, n)
kernel_name = 'mk_dlrm_tower_d1_rec_r8_1a7abc'

def setup_inputs(seed: int=0):
    np.random.seed(seed)
    _w = jnp.asarray

    def _rec_inputs():
        import jax
        import jax.numpy as jnp
        _tk = jax.random.key(seed)
        dense_ctx = jax.random.normal(jax.random.fold_in(_tk, 190), (512, 16), jnp.float32)
        ids = jnp.stack([jax.random.randint(jax.random.fold_in(_tk, 200 + f), (512,), 0, v, jnp.int32) for f, v in enumerate([12500, 12500, 1250, 1250, 1000, 1000, 1250, 125000, 12500, 1250, 1250, 1000, 1250, 1250, 125000, 1000, 12500, 1250, 1250, 125000, 125000, 1250, 12500, 12500, 125000, 12500, 12500, 12500, 1250, 125000, 12500, 125000, 1000, 1000, 125000, 1250, 125000, 125000, 12500])], axis=1)
        tbl_0 = 0.05 * jax.random.normal(jax.random.fold_in(_tk, 500 + 0), (12500, 16), jnp.float32)
        tbl_1 = 0.05 * jax.random.normal(jax.random.fold_in(_tk, 500 + 1), (12500, 16), jnp.float32)
        tbl_2 = 0.05 * jax.random.normal(jax.random.fold_in(_tk, 500 + 2), (1250, 16), jnp.float32)
        tbl_3 = 0.05 * jax.random.normal(jax.random.fold_in(_tk, 500 + 3), (1250, 16), jnp.float32)
        tbl_4 = 0.05 * jax.random.normal(jax.random.fold_in(_tk, 500 + 4), (1000, 16), jnp.float32)
        tbl_5 = 0.05 * jax.random.normal(jax.random.fold_in(_tk, 500 + 5), (1000, 16), jnp.float32)
        tbl_6 = 0.05 * jax.random.normal(jax.random.fold_in(_tk, 500 + 6), (1250, 16), jnp.float32)
        tbl_7 = 0.05 * jax.random.normal(jax.random.fold_in(_tk, 500 + 7), (125000, 16), jnp.float32)
        tbl_8 = 0.05 * jax.random.normal(jax.random.fold_in(_tk, 500 + 8), (12500, 16), jnp.float32)
        tbl_9 = 0.05 * jax.random.normal(jax.random.fold_in(_tk, 500 + 9), (1250, 16), jnp.float32)
        tbl_10 = 0.05 * jax.random.normal(jax.random.fold_in(_tk, 500 + 10), (1250, 16), jnp.float32)
        tbl_11 = 0.05 * jax.random.normal(jax.random.fold_in(_tk, 500 + 11), (1000, 16), jnp.float32)
        tbl_12 = 0.05 * jax.random.normal(jax.random.fold_in(_tk, 500 + 12), (1250, 16), jnp.float32)
        tbl_13 = 0.05 * jax.random.normal(jax.random.fold_in(_tk, 500 + 13), (1250, 16), jnp.float32)
        tbl_14 = 0.05 * jax.random.normal(jax.random.fold_in(_tk, 500 + 14), (125000, 16), jnp.float32)
        tbl_15 = 0.05 * jax.random.normal(jax.random.fold_in(_tk, 500 + 15), (1000, 16), jnp.float32)
        tbl_16 = 0.05 * jax.random.normal(jax.random.fold_in(_tk, 500 + 16), (12500, 16), jnp.float32)
        tbl_17 = 0.05 * jax.random.normal(jax.random.fold_in(_tk, 500 + 17), (1250, 16), jnp.float32)
        tbl_18 = 0.05 * jax.random.normal(jax.random.fold_in(_tk, 500 + 18), (1250, 16), jnp.float32)
        tbl_19 = 0.05 * jax.random.normal(jax.random.fold_in(_tk, 500 + 19), (125000, 16), jnp.float32)
        tbl_20 = 0.05 * jax.random.normal(jax.random.fold_in(_tk, 500 + 20), (125000, 16), jnp.float32)
        tbl_21 = 0.05 * jax.random.normal(jax.random.fold_in(_tk, 500 + 21), (1250, 16), jnp.float32)
        tbl_22 = 0.05 * jax.random.normal(jax.random.fold_in(_tk, 500 + 22), (12500, 16), jnp.float32)
        tbl_23 = 0.05 * jax.random.normal(jax.random.fold_in(_tk, 500 + 23), (12500, 16), jnp.float32)
        tbl_24 = 0.05 * jax.random.normal(jax.random.fold_in(_tk, 500 + 24), (125000, 16), jnp.float32)
        tbl_25 = 0.05 * jax.random.normal(jax.random.fold_in(_tk, 500 + 25), (12500, 16), jnp.float32)
        tbl_26 = 0.05 * jax.random.normal(jax.random.fold_in(_tk, 500 + 26), (12500, 16), jnp.float32)
        tbl_27 = 0.05 * jax.random.normal(jax.random.fold_in(_tk, 500 + 27), (12500, 16), jnp.float32)
        tbl_28 = 0.05 * jax.random.normal(jax.random.fold_in(_tk, 500 + 28), (1250, 16), jnp.float32)
        tbl_29 = 0.05 * jax.random.normal(jax.random.fold_in(_tk, 500 + 29), (125000, 16), jnp.float32)
        tbl_30 = 0.05 * jax.random.normal(jax.random.fold_in(_tk, 500 + 30), (12500, 16), jnp.float32)
        tbl_31 = 0.05 * jax.random.normal(jax.random.fold_in(_tk, 500 + 31), (125000, 16), jnp.float32)
        tbl_32 = 0.05 * jax.random.normal(jax.random.fold_in(_tk, 500 + 32), (1000, 16), jnp.float32)
        tbl_33 = 0.05 * jax.random.normal(jax.random.fold_in(_tk, 500 + 33), (1000, 16), jnp.float32)
        tbl_34 = 0.05 * jax.random.normal(jax.random.fold_in(_tk, 500 + 34), (125000, 16), jnp.float32)
        tbl_35 = 0.05 * jax.random.normal(jax.random.fold_in(_tk, 500 + 35), (1250, 16), jnp.float32)
        tbl_36 = 0.05 * jax.random.normal(jax.random.fold_in(_tk, 500 + 36), (125000, 16), jnp.float32)
        tbl_37 = 0.05 * jax.random.normal(jax.random.fold_in(_tk, 500 + 37), (125000, 16), jnp.float32)
        tbl_38 = 0.05 * jax.random.normal(jax.random.fold_in(_tk, 500 + 38), (12500, 16), jnp.float32)
        _rk = jax.random.fold_in(_tk, 7)
        W_top1 = 0.05 * jax.random.normal(jax.random.fold_in(_tk, 801), (400, 512), jnp.float32)
        W_top2 = 0.0441942 * jax.random.normal(jax.random.fold_in(_tk, 802), (512, 256), jnp.float32)
        W_top3 = 0.0625 * jax.random.normal(jax.random.fold_in(_tk, 803), (256, 1), jnp.float32)
        b_top1 = jnp.zeros((512,), jnp.float32)
        b_top2 = jnp.zeros((256,), jnp.float32)
        return (dense_ctx, ids, tbl_0, tbl_1, tbl_2, tbl_3, tbl_4, tbl_5, tbl_6, tbl_7, tbl_8, tbl_9, tbl_10, tbl_11, tbl_12, tbl_13, tbl_14, tbl_15, tbl_16, tbl_17, tbl_18, tbl_19, tbl_20, tbl_21, tbl_22, tbl_23, tbl_24, tbl_25, tbl_26, tbl_27, tbl_28, tbl_29, tbl_30, tbl_31, tbl_32, tbl_33, tbl_34, tbl_35, tbl_36, tbl_37, tbl_38, W_top1, b_top1, W_top2, b_top2, W_top3)
    dense_ctx, ids, tbl_0, tbl_1, tbl_2, tbl_3, tbl_4, tbl_5, tbl_6, tbl_7, tbl_8, tbl_9, tbl_10, tbl_11, tbl_12, tbl_13, tbl_14, tbl_15, tbl_16, tbl_17, tbl_18, tbl_19, tbl_20, tbl_21, tbl_22, tbl_23, tbl_24, tbl_25, tbl_26, tbl_27, tbl_28, tbl_29, tbl_30, tbl_31, tbl_32, tbl_33, tbl_34, tbl_35, tbl_36, tbl_37, tbl_38, W_top1, b_top1, W_top2, b_top2, W_top3 = _rec_inputs()

    def _L0_rec_setup():
        import jax, jax.numpy as jnp
        import numpy as np
        B, F0, D = (512, 39, 16)
        CIN = [128, 128, 128]

        def _cin_layer(X0, Xi, W, b):
            H = W.shape[0]
            F0_, Fi = (X0.shape[1], Xi.shape[1])
            Wr = W.reshape(H, F0_, Fi)
            return jnp.einsum('hjk,bjd,bkd->bhd', Wr, X0, Xi) + b[None, :, None]
        key = jax.random.key(seed)
        ks = jax.random.split(key, 4)
        x = jax.random.normal(ks[0], (B, F0, D), dtype=jnp.float32)
        fields = [F0] + CIN
        inp = {'embedded_features': x}
        for i in range(len(CIN)):
            cin = F0 * fields[i]
            cout = fields[i + 1]
            kw = jax.random.fold_in(ks[1], i)
            inp[f'W{i}'] = jax.random.normal(kw, (cout, cin), dtype=jnp.float32) / np.sqrt(cin)
            inp[f'b{i}'] = jnp.zeros((cout,), dtype=jnp.float32)
        return inp
    _L0_rec_all = _L0_rec_setup()
    _L0_rec_in = {k: v for k, v in _L0_rec_all.items() if k in ('W0', 'b0', 'W1', 'b1', 'W2', 'b2')}
    del _L0_rec_all
    return {'dense_ctx': dense_ctx, 'ids': ids, 'tbl_0': tbl_0, 'tbl_1': tbl_1, 'tbl_2': tbl_2, 'tbl_3': tbl_3, 'tbl_4': tbl_4, 'tbl_5': tbl_5, 'tbl_6': tbl_6, 'tbl_7': tbl_7, 'tbl_8': tbl_8, 'tbl_9': tbl_9, 'tbl_10': tbl_10, 'tbl_11': tbl_11, 'tbl_12': tbl_12, 'tbl_13': tbl_13, 'tbl_14': tbl_14, 'tbl_15': tbl_15, 'tbl_16': tbl_16, 'tbl_17': tbl_17, 'tbl_18': tbl_18, 'tbl_19': tbl_19, 'tbl_20': tbl_20, 'tbl_21': tbl_21, 'tbl_22': tbl_22, 'tbl_23': tbl_23, 'tbl_24': tbl_24, 'tbl_25': tbl_25, 'tbl_26': tbl_26, 'tbl_27': tbl_27, 'tbl_28': tbl_28, 'tbl_29': tbl_29, 'tbl_30': tbl_30, 'tbl_31': tbl_31, 'tbl_32': tbl_32, 'tbl_33': tbl_33, 'tbl_34': tbl_34, 'tbl_35': tbl_35, 'tbl_36': tbl_36, 'tbl_37': tbl_37, 'tbl_38': tbl_38, 'W_top1': W_top1, 'b_top1': b_top1, 'W_top2': W_top2, 'b_top2': b_top2, 'W_top3': W_top3, 'L0_rec_W0': _L0_rec_in['W0'], 'L0_rec_b0': _L0_rec_in['b0'], 'L0_rec_W1': _L0_rec_in['W1'], 'L0_rec_b1': _L0_rec_in['b1'], 'L0_rec_W2': _L0_rec_in['W2'], 'L0_rec_b2': _L0_rec_in['b2']}

def reference(dense_ctx, ids, tbl_0, tbl_1, tbl_2, tbl_3, tbl_4, tbl_5, tbl_6, tbl_7, tbl_8, tbl_9, tbl_10, tbl_11, tbl_12, tbl_13, tbl_14, tbl_15, tbl_16, tbl_17, tbl_18, tbl_19, tbl_20, tbl_21, tbl_22, tbl_23, tbl_24, tbl_25, tbl_26, tbl_27, tbl_28, tbl_29, tbl_30, tbl_31, tbl_32, tbl_33, tbl_34, tbl_35, tbl_36, tbl_37, tbl_38, W_top1, b_top1, W_top2, b_top2, W_top3, L0_rec_W0, L0_rec_b0, L0_rec_W1, L0_rec_b1, L0_rec_W2, L0_rec_b2):
    import jax
    import jax.numpy as jnp

    def _L0_rec_ref(embedded_features, W0, b0, W1, b1, W2, b2):
        import jax, jax.numpy as jnp
        import numpy as np
        B, F0, D = (512, 39, 16)
        CIN = [128, 128, 128]

        def _cin_layer(X0, Xi, W, b):
            H = W.shape[0]
            F0_, Fi = (X0.shape[1], Xi.shape[1])
            Wr = W.reshape(H, F0_, Fi)
            return jnp.einsum('hjk,bjd,bkd->bhd', Wr, X0, Xi) + b[None, :, None]
        X0 = embedded_features
        Ws = [(W0, b0), (W1, b1), (W2, b2)]
        Xi = X0
        res = []
        for W, b in Ws:
            Xi = _cin_layer(X0, Xi, W, b)
            res.append(Xi.sum(axis=2))
        return jnp.concatenate(res, axis=1)
    e = jnp.stack([tbl_0[ids[:, 0]], tbl_1[ids[:, 1]], tbl_2[ids[:, 2]], tbl_3[ids[:, 3]], tbl_4[ids[:, 4]], tbl_5[ids[:, 5]], tbl_6[ids[:, 6]], tbl_7[ids[:, 7]], tbl_8[ids[:, 8]], tbl_9[ids[:, 9]], tbl_10[ids[:, 10]], tbl_11[ids[:, 11]], tbl_12[ids[:, 12]], tbl_13[ids[:, 13]], tbl_14[ids[:, 14]], tbl_15[ids[:, 15]], tbl_16[ids[:, 16]], tbl_17[ids[:, 17]], tbl_18[ids[:, 18]], tbl_19[ids[:, 19]], tbl_20[ids[:, 20]], tbl_21[ids[:, 21]], tbl_22[ids[:, 22]], tbl_23[ids[:, 23]], tbl_24[ids[:, 24]], tbl_25[ids[:, 25]], tbl_26[ids[:, 26]], tbl_27[ids[:, 27]], tbl_28[ids[:, 28]], tbl_29[ids[:, 29]], tbl_30[ids[:, 30]], tbl_31[ids[:, 31]], tbl_32[ids[:, 32]], tbl_33[ids[:, 33]], tbl_34[ids[:, 34]], tbl_35[ids[:, 35]], tbl_36[ids[:, 36]], tbl_37[ids[:, 37]], tbl_38[ids[:, 38]]], axis=1)
    z = _L0_rec_ref(e, L0_rec_W0, L0_rec_b0, L0_rec_W1, L0_rec_b1, L0_rec_W2, L0_rec_b2)
    z = z.reshape(z.shape[0], -1)
    h = jnp.concatenate([z, dense_ctx], axis=1)
    h = jnp.maximum(h @ W_top1 + b_top1, 0.0)
    h = jnp.maximum(h @ W_top2 + b_top2, 0.0)
    y = h @ W_top3
    return y

_drawn_inputs = setup_inputs


def setup_inputs(seed=0):
    import zlib

    import numpy as np

    out = dict(_drawn_inputs(seed))
    spreads = {'b_top1': (0.0, 0.1),
     'b_top2': (0.0, 0.1),
     'L0_rec_b0': (0.0, 0.1),
     'L0_rec_b1': (0.0, 0.1),
     'L0_rec_b2': (0.0, 0.1)}
    factors = {'tbl_0': 8.0,
     'tbl_1': 6.044,
     'tbl_2': 5.394,
     'tbl_3': 6.985,
     'tbl_4': 8.0,
     'tbl_5': 8.0,
     'tbl_6': 8.0,
     'tbl_7': 6.726,
     'tbl_8': 8.0,
     'tbl_9': 8.0,
     'tbl_10': 8.0,
     'tbl_11': 7.367,
     'tbl_12': 8.0,
     'tbl_13': 8.0,
     'tbl_14': 4.554,
     'tbl_15': 5.588,
     'tbl_16': 8.0,
     'tbl_17': 8.0,
     'tbl_18': 8.0,
     'tbl_19': 5.905,
     'tbl_20': 7.37,
     'tbl_21': 8.0,
     'tbl_22': 8.0,
     'tbl_23': 8.0,
     'tbl_24': 8.0,
     'tbl_25': 7.112,
     'tbl_26': 6.147,
     'tbl_27': 8.0,
     'tbl_28': 8.0,
     'tbl_29': 8.0,
     'tbl_30': 6.398,
     'tbl_31': 6.661,
     'tbl_32': 8.0,
     'tbl_33': 6.108,
     'tbl_34': 8.0,
     'tbl_35': 7.383,
     'tbl_36': 8.0,
     'tbl_37': 6.614,
     'tbl_38': 8.0,
     'L0_rec_W0': 3.207}
    for name, (base, spread) in spreads.items():
        noise = np.random.default_rng([zlib.crc32(name.encode()), seed]).standard_normal(out[name].shape)
        drawn = base * np.exp(spread * noise) if base else spread * noise
        out[name] = jnp.asarray(drawn.astype(out[name].dtype))
    for name, factor in factors.items():
        out[name] = (out[name] * factor).astype(out[name].dtype)
    return out
```

```python
from contextlib import ExitStack

import numpy as np

import concourse.bass as bass
from concourse import mybir

F32 = mybir.dt.float32
BF16 = mybir.dt.bfloat16
I32 = mybir.dt.int32
U32 = mybir.dt.uint32
ALU = mybir.AluOpType
ACT = mybir.ActivationFunctionType
AX = mybir.AxisListType

P = 128
B, F, D, H = 512, 39, 16, 128
PARTS = 3
KX = PARTS * F
TILES = B // P
CB = 32
COLS = CB * D
CHUNKS = B // CB
QPT = P // CB
DQ = 4
UNITS = TILES * D // DQ
GB = 8
GROUPS = CB // GB
R0 = F + 1
K0 = 3 * R0
T0 = (F // 2 + 1 + 2) // 3
ROTW = P + F - 1
HID1, HID2, DENSE = 512, 256, 16

C_ROT, C_SEL, C_MASK, C_ID = 0, ROTW, ROTW + K0, ROTW + K0 + GB
C_ALL = C_ID + P

FULL = UNITS - QPT - 1
L0_AFTER = (3, 8, 13, 18, 23, 28, 33)
STEPS_NEXT = []
for _s in range(F):
    STEPS_NEXT.append((1, _s))
    if _s in L0_AFTER:
        STEPS_NEXT.append((0, L0_AFTER.index(_s)))
STEPS_LAST = [(1, s) for s in range(F)]
NSTEP = len(STEPS_NEXT)
TURN_AFTER, PREP_AFTER, G_AFTER = 2, 30, (10, 15, 20, 25)


def first_step(c):
    return T0 + NSTEP * c


def wait_done(engine, semaphore, count):
    if not (isinstance(count, int) and count <= 0):
        engine.wait_ge(semaphore, count)


def build(nc, a):
    ctx = ExitStack()
    with ctx:
        def sb(name, shape, dt=F32):
            return ctx.enter_context(nc.sbuf_tensor(name, shape, dt))

        def ps(name, shape=(P, 512), dt=F32):
            return ctx.enter_context(nc.psum_tensor(name, list(shape), dt))

        def sem(name):
            return ctx.enter_context(nc.semaphore(name))

        const = sb("const", [P, C_ALL])
        rot = sb("rot", [KX, ROTW], BF16)
        sel = sb("sel", [KX, K0], BF16)
        ident = sb("ident", [P, P], BF16)
        ids = sb("ids", [P, TILES, F], I32)
        emb = sb("emb", [P, 2, F * D])
        rest = sb("rest", [P, D, F])
        parts_flat = sb("parts", [P, TILES * D * KX], BF16)
        parts = parts_flat[:, :].rearrange("p (t d k) -> p t d k", t=TILES, d=D)
        xs = sb("xs", [KX, TILES, P // GB, D // DQ, DQ * GB], BF16)
        w0 = sb("w0", [K0, T0, H])
        w1 = sb("w1", [P, F, H])
        w2 = sb("w2", [P, F, H])
        x0a = sb("x0a", [K0, COLS])
        x1 = sb("x1", [P, 2 * COLS])
        x2 = sb("x2", [P, COLS])
        x2t = sb("x2t", [P, GROUPS, H])
        diag = sb("diag", [P, GROUPS, GB, F])
        prod = sb("prod", [P, 2, COLS])
        gram = sb("gram", [P, F, B])
        z = sb("z", [P, 3, B])
        wt1 = sb("wt1", [P, 3, HID1])
        wt1d = sb("wt1d", [DENSE, HID1])
        dense = sb("dense", [DENSE, B])
        wt2 = sb("wt2", [P, HID1 // P, HID2])
        wt3 = sb("wt3", [P, HID2 // P])
        bias = sb("bias", [P, 3])
        bias2d = sb("bias2d", [P, 1])
        bt1 = sb("bt1", [P, HID1 // P])
        bt2 = sb("bt2", [P, HID2 // P])
        y = sb("y", [1, B])
        w0ab = gram[:, 0:4, :].rearrange("p a b -> p (a b)")[:, 0:2 * T0 * H].rearrange(
            "p (a n) -> p a n", a=2)
        spent = parts_flat[:, :].bitcast(F32)
        h1 = spent[:, 0:4 * B].rearrange("p (m b) -> p m b", m=4)
        h2 = emb[:, :, :].rearrange("p a n -> p (a n)")[:, 0:2 * B].rearrange("p (m b) -> p m b", m=2)

        spread = [ps("spread0"), ps("spread1")]
        acc0, acc1 = ps("acc0"), ps("acc1")
        misc0, misc1 = ps("misc0"), ps("misc1")
        gps = [ps("gps0"), ps("gps1")]

        ids_in, const_in, w0_in, w1_in, w2_in = (sem(n) for n in ("ids_in", "const_in", "w0_in", "w1_in", "w2_in"))
        bias_in, mlp_in, out_done = sem("bias_in"), sem("mlp_in"), sem("out_done")
        gathered = [sem(f"gathered{t}") for t in range(TILES)]
        bias2d_ready = sem("bias2d_ready")
        const_ready = sem("const_ready")
        w0_ready = sem("w0_ready")
        split_step = sem("split_step")
        parts_ready = sem("parts_ready")
        unit_done, xs_ready = sem("unit_done"), sem("xs_ready")
        base_done, x0a_ready = sem("base_done"), sem("x0a_ready")
        spread_ready = sem("spread_ready")
        prod_ready = sem("prod_ready")
        main_done = sem("main_done")
        x1_ready, x2_ready = sem("x1_ready"), sem("x2_ready")
        x0t_done, diag_ready = sem("x0t_done"), sem("diag_ready")
        x2t_done, x2t_ready = sem("x2t_done"), sem("x2t_ready")
        g_done, g_ready = sem("g_done"), sem("g_ready")
        z_sums = sem("z_sums")
        tail_mm, tail_act = sem("tail_mm"), sem("tail_act")

        def chunk_cols(c):
            return xs[:, :, :, :, :].rearrange("p t q e r -> p (t q e r)")[:, bass.ds(c * COLS, COLS)]

        block = ctx.enter_context(nc.Block())

        @block.sync
        def _(sp):
            sp.dma_start(ids[:, :, :], a["ids"].rearrange("(t p) f -> p t f", p=P)).then_inc(ids_in, 16)
            sp.dma_start(const[:, :], a["const"]).then_inc(const_in, 16)
            sp.dma_start(w0ab[0:K0], a["w0ab"]).then_inc(w0_in, 16)
            for i in range(3):
                sp.dma_start(bias[:, i:i + 1], a[f"b{i}"].rearrange("(p o) -> p o", o=1)).then_inc(bias_in, 16)
            sp.dma_start(w1[:, :, :], a["w1"]).then_inc(w1_in, 16)
            sp.dma_start(w2[:, :, :], a["w2"]).then_inc(w2_in, 16)
            sp.dma_start(wt1[:, :, :], a["W_top1"][0:3 * H, :].rearrange("(i p) n -> p i n", p=P)).then_inc(mlp_in, 16)
            sp.dma_start(wt1d[:, :], a["W_top1"][3 * H:, :]).then_inc(mlp_in, 16)
            sp.dma_start(dense[:, :], a["dense_t"]).then_inc(mlp_in, 16)
            sp.dma_start(wt2[:, :, :], a["W_top2"].rearrange("(i p) n -> p i n", p=P)).then_inc(mlp_in, 16)
            sp.dma_start(wt3[:, :], a["w_top3"]).then_inc(mlp_in, 16)
            sp.dma_start(bt1[:, :], a["b_top1"]).then_inc(mlp_in, 16)
            sp.dma_start(bt2[:, :], a["b_top2"]).then_inc(mlp_in, 16)
            sp.wait_ge(tail_act, 8)
            sp.dma_start(a["out"].rearrange("b o -> o b"), y[:, :]).then_inc(out_done, 16)
            sp.wait_ge(out_done, 16)

        @block.gpsimd
        def _(pool):
            pool.wait_ge(ids_in, 16)
            for t in range(TILES):
                if t >= 2:
                    pool.wait_ge(parts_ready, t - 1)
                for f in range(F):
                    pool.indirect_dma_start(
                        emb[:, t % 2, f * D:(f + 1) * D], None, a[f"tbl_{f}"],
                        bass.IndirectOffsetOnAxis(ap=ids[:, t, f:f + 1].bitcast(U32), axis=0),
                    ).then_inc(gathered[t], 16)
                pool.wait_ge(gathered[t], 16 * F)
                e = emb[:, t % 2, :].rearrange("p (f d) -> p d f", f=F)
                part = [parts[:, t, :, i * F:(i + 1) * F] for i in range(PARTS)]
                pool.tensor_copy(part[0], e).then_inc(split_step, 1)
                pool.wait_ge(split_step, 3 * t + 1)
                if t:
                    pool.wait_ge(parts_ready, t)
                pool.tensor_tensor(rest[:, :, :], e, part[0], ALU.subtract).then_inc(split_step, 1)
                pool.wait_ge(split_step, 3 * t + 2)
                pool.tensor_copy(part[1], rest[:, :, :]).then_inc(split_step, 1)
                pool.wait_ge(split_step, 3 * t + 3)
                pool.tensor_tensor(part[2], rest[:, :, :], part[1], ALU.subtract).then_inc(parts_ready, 1)

        @block.tensor
        def _(pe):
            def lay_out(w, after):
                pe.wait_ge(parts_ready, (w >> 2) + 1)
                if after is not None:
                    pe.wait_ge(xs_ready, after)
                for i in range(DQ):
                    lhs = parts_flat[
                        :, bass.ds((w * DQ + i) * KX, KX)]
                    mm = pe.matmul(misc1[0:KX, i * P:(i + 1) * P], lhs, ident[:, :], start=True, stop=True)
                mm.then_inc(unit_done, 1)

            def base(c):
                pe.matmul(misc0[0:K0, :], sel[:, :], chunk_cols(c), start=True, stop=True).then_inc(base_done, 1)

            def spread_x0(layer, k, c, buf):
                m, shift = (P, k) if layer else (K0, 3 * k)
                pe.matmul(spread[buf][0:m, :], rot[:, shift:shift + m], chunk_cols(c),
                          start=True, stop=True).then_inc(spread_ready, 1)

            def contract(layer, k, buf):
                if layer:
                    mm = pe.matmul(acc1[:, :], w1[:, k, :], prod[:, buf, :], start=(k == 0), stop=(k == F - 1))
                else:
                    mm = pe.matmul(acc0[:, :], w0[:, k, :], prod[0:K0, buf, :], start=(k == 0), stop=(k == T0 - 1))
                mm.then_inc(main_done, 1)

            def x0_turned(c):
                v = chunk_cols(c).rearrange("p (g n) -> p g n", g=GROUPS)
                for g in range(GROUPS):
                    mm = pe.matmul(misc1[:, g * F:(g + 1) * F], v[:, g], rot[:, 0:F], start=True, stop=True)
                mm.then_inc(x0t_done, 1)

            def x2_turned(c):
                v = x2[:, :].rearrange("p (g n) -> p g n", g=GROUPS)
                for g in range(GROUPS):
                    mm = pe.transpose(misc0[:, g * H:(g + 1) * H], v[:, g], const[:, C_ID:C_ID + P])
                mm.then_inc(x2t_done, 1)

            def gram_group(c, g):
                if g == 0:
                    pe.wait_ge(x2t_ready, c + 1)
                    pe.wait_ge(diag_ready, c + 1)
                wait_done(pe, g_ready, GROUPS * c if g < 2 else GROUPS * c + g - 1)
                pe.matmul(gps[g % 2][:, 0:GB * F], x2t[:, g, :],
                          diag[:, g, :, :].rearrange("p b j -> p (b j)"), start=True, stop=True).then_inc(g_done, 1)

            def chunk(c, prev, nxt, laid, units):
                steps = STEPS_NEXT if nxt else STEPS_LAST
                n0 = first_step(c)
                if nxt:
                    pe.wait_ge(xs_ready, (((c + 1) >> 2) << 2) + 4)
                    if prev:
                        wait_done(pe, x2t_ready, c - 1)
                    base(c + 1)
                if prev:
                    pe.wait_ge(xs_ready, laid)
                    x0_turned(c - 1)
                for i, (layer, k) in enumerate(steps):
                    buf = (T0 + i) % 2
                    pe.wait_ge(prod_ready, n0 + i + 1)
                    if i + 2 < len(steps):
                        l2, k2 = steps[i + 2]
                        spread_x0(l2, k2, c if l2 else c + 1, buf)
                    elif nxt:
                        spread_x0(1, i + 2 - len(steps), c + 1, buf)
                    if layer and k == 0 and prev:
                        pe.wait_ge(x2_ready, c)
                    if not layer and k == 0:
                        pe.wait_ge(x1_ready, c + 1)
                    contract(layer, k, buf)
                    if not layer:
                        continue
                    if prev and k == TURN_AFTER:
                        if nxt:
                            pe.wait_ge(x0a_ready, c + 2)
                        x2_turned(c - 1)
                    if prev and k in G_AFTER:
                        gram_group(c - 1, G_AFTER.index(k))
                    if k == PREP_AFTER:
                        for j, w in enumerate(units):
                            if prev:
                                pe.wait_ge(diag_ready, c)
                            lay_out(w, w if j else None)

            pe.wait_ge(const_ready, 3)
            for w in range(QPT):
                lay_out(w, w if w else None)
            pe.wait_ge(xs_ready, QPT)
            base(0)
            steps = [(0, k) for k in range(T0)] + [(1, 0), (1, 1)]
            for i in range(2):
                spread_x0(*steps[i], 0, i)
            pe.wait_ge(w0_ready, 1)
            for i in range(T0):
                pe.wait_ge(prod_ready, i + 1)
                spread_x0(*steps[i + 2], 0, i % 2)
                contract(0, i, i % 2)
            pe.wait_ge(w1_in, 16)
            chunk(0, False, True, QPT, [QPT, QPT + 1])
            chunk(1, True, True, QPT + 2, [QPT + 2])
            with pe.Fori(2, FULL) as c:
                chunk(c, True, True, c + QPT + 1, [c + QPT + 1])
            with pe.Fori(FULL, CHUNKS - 1) as c:
                chunk(c, True, True, UNITS, [])
            chunk(CHUNKS - 1, True, False, UNITS, [])

            x0_turned(CHUNKS - 1)
            pe.wait_ge(x2_ready, CHUNKS)
            x2_turned(CHUNKS - 1)
            for g in range(GROUPS):
                gram_group(CHUNKS - 1, g)
            pe.wait_ge(w2_in, 16)
            pe.wait_ge(g_ready, GROUPS * CHUNKS)
            for j in range(F):
                mm = pe.matmul(acc1[:, :], w2[:, j, :], gram[:, j, :], start=(j == 0), stop=(j == F - 1))
            mm.then_inc(tail_mm, 1)
            pe.wait_ge(mlp_in, 7 * 16)
            pe.wait_ge(z_sums, 2 * CHUNKS)
            pe.wait_ge(diag_ready, CHUNKS)
            hid = [acc0, misc0, misc1, gps[0]]
            for m in range(HID1 // P):
                cols = slice(m * P, (m + 1) * P)
                pe.matmul(hid[m][:, :], wt1[:, 0, cols], z[:, 0, :], start=True, stop=False)
                pe.matmul(hid[m][:, :], wt1[:, 1, cols], z[:, 1, :], start=False, stop=False)
                pe.matmul(hid[m][:, :], wt1d[:, cols], dense[:, :], start=False, stop=False)
            pe.wait_ge(tail_act, 1)
            for m in range(HID1 // P):
                cols = slice(m * P, (m + 1) * P)
                pe.matmul(hid[m][:, :], wt1[:, 2, cols], z[:, 2, :], start=False, stop=True).then_inc(tail_mm, 1)
            hid2 = [gps[1], spread[0]]
            for i in range(HID1 // P):
                pe.wait_ge(tail_act, 2 + i)
                for m in range(HID2 // P):
                    mm = pe.matmul(hid2[m][:, :], wt2[:, i, m * P:(m + 1) * P], h1[:, i, :],
                                   start=(i == 0), stop=(i == HID1 // P - 1))
                    if i == HID1 // P - 1:
                        mm.then_inc(tail_mm, 1)
            for i in range(HID2 // P):
                pe.wait_ge(tail_act, 6 + i)
                mm = pe.matmul(spread[1][0:1, :], wt3[:, i:i + 1], h2[:, i, :],
                               start=(i == 0), stop=(i == HID2 // P - 1))
            mm.then_inc(tail_mm, 1)

        @block.vector
        def _(dve):
            def product(layer, c, n, buf):
                dve.wait_ge(spread_ready, n + 1)
                dve.wait_ge(main_done, n - 1)
                m = P if layer else K0
                other = x1[:, bass.ds((c & 1) * COLS, COLS)] if layer else x0a[:, :]
                dve.tensor_tensor(prod[0:m, buf, :], spread[buf][0:m, :], other, ALU.mult).then_inc(prod_ready, 1)

            def sum_dims(layer, c, src):
                dve.tensor_reduce(z[:, layer, bass.ds(c * CB, CB)].rearrange("p (g b) -> p g b", g=GROUPS),
                                  src.rearrange("p (g d b) -> p g b d", g=GROUPS, d=D), AX.X, ALU.add).then_inc(z_sums, 1)

            def block_diagonal(c):
                dve.wait_ge(x0t_done, c + 1)
                wait_done(dve, g_done, GROUPS * c)
                turned = misc1[:, 0:GROUPS * F].rearrange("p (g o j) -> p g o j", g=GROUPS, o=1)
                mask = const[:, C_MASK:C_MASK + GB].rearrange("p (g b o) -> p g b o", g=1, o=1)
                dve.tensor_tensor(diag[:, :, :, :], turned.to_broadcast([P, GROUPS, GB, F]),
                                  mask.to_broadcast([P, GROUPS, GB, F]), ALU.mult).then_inc(diag_ready, 1)

            def chunk(c, prev, nxt):
                steps = STEPS_NEXT if nxt else STEPS_LAST
                for i, (layer, k) in enumerate(steps):
                    if layer and k == 0:
                        dve.wait_ge(x1_ready, c + 1)
                    if not layer and k == 0:
                        dve.wait_ge(x0a_ready, c + 2)
                    product(layer, c, first_step(c) + i, (T0 + i) % 2)
                    if layer and k == 0 and prev:
                        block_diagonal(c - 1)
                    if layer and k == 1 and prev:
                        dve.wait_ge(x2_ready, c)
                        sum_dims(1, c - 1, x2[:, :])
                    if layer and k == 5:
                        sum_dims(0, c, x1[:, bass.ds((c & 1) * COLS, COLS)])

            dve.wait_ge(w0_in, 16)
            dve.tensor_tensor(w0[:, :, :].rearrange("p s h -> p (s h)"), w0ab[0:K0, 0], w0ab[0:K0, 1],
                              ALU.add).then_inc(w0_ready, 1)
            dve.wait_ge(const_in, 16)
            dve.wait_ge(x0a_ready, 1)
            for i in range(T0):
                dve.wait_ge(spread_ready, i + 1)
                if i >= 2:
                    dve.wait_ge(main_done, i - 1)
                dve.tensor_tensor(prod[0:K0, i % 2, :], spread[i % 2][0:K0, :], x0a[:, :],
                                  ALU.mult).then_inc(prod_ready, 1)
            chunk(0, False, True)
            chunk(1, True, True)
            with dve.Fori(2, CHUNKS - 1) as c:
                chunk(c, True, True)
            chunk(CHUNKS - 1, True, False)
            block_diagonal(CHUNKS - 1)
            dve.wait_ge(x2_ready, CHUNKS)
            sum_dims(1, CHUNKS - 1, x2[:, :])

        @block.scalar
        def _(act):
            def evacuate_unit(w):
                act.wait_ge(unit_done, w + 1)
                tile = w // QPT if isinstance(w, int) else (w >> 2).with_bounds(min_val=0, max_val=TILES - 1)
                dst = xs[:, bass.ds(tile, 1), :, bass.ds(w & 3, 1), :]
                act.activation(dst.rearrange("p t q e (d b) -> p (t q e) d b", d=DQ),
                               misc1[0:KX, :].rearrange("p (d q b) -> p q d b", d=DQ, b=GB),
                               ACT.Copy).then_inc(xs_ready, 1)

            def evacuate_base(c):
                act.wait_ge(base_done, c + 1)
                act.activation(x0a[:, :], misc0[0:K0, :], ACT.Copy).then_inc(x0a_ready, 1)

            def evacuate_x1(c, steps_done):
                act.wait_ge(main_done, steps_done)
                act.activation(x1[:, bass.ds((c & 1) * COLS, COLS)], acc0[:, :], ACT.Identity,
                               bias=bias[:, 0:1]).then_inc(x1_ready, 1)

            def evacuate_x2(c):
                act.wait_ge(main_done, first_step(c + 1) if not isinstance(c, int) or c < CHUNKS - 1
                            else first_step(c) + len(STEPS_LAST))
                wait_done(act, x2t_done, c)
                wait_done(act, z_sums, 2 * c)
                act.activation(x2[:, :], acc1[:, :], ACT.Identity, bias=bias[:, 1:2]).then_inc(x2_ready, 1)

            def evacuate_turned(c):
                act.wait_ge(x2t_done, c + 1)
                act.activation(x2t[:, :, :].rearrange("p g h -> p (g h)"), misc0[:, :],
                               ACT.Copy).then_inc(x2t_ready, 1)

            def evacuate_gram(c, g):
                act.wait_ge(g_done, GROUPS * c + g + 1)
                act.activation(gram[:, :, bass.ds(c * CB + g * GB, GB)],
                               gps[g % 2][:, 0:GB * F].rearrange("p (b j) -> p j b", b=GB),
                               ACT.Copy).then_inc(g_ready, 1)

            def chunk(c, prev, nxt, units):
                if prev:
                    evacuate_x2(c - 1)
                if nxt:
                    evacuate_base(c + 1)
                if prev:
                    evacuate_turned(c - 1)
                    for g in range(GROUPS):
                        evacuate_gram(c - 1, g)
                for w in units:
                    evacuate_unit(w)
                if nxt:
                    last_l0 = max(i for i, (layer, _) in enumerate(STEPS_NEXT) if not layer)
                    evacuate_x1(c + 1, first_step(c) + last_l0 + 1)

            act.wait_ge(const_in, 16)
            act.activation(rot[:, :], const[0:KX, C_ROT:C_ROT + ROTW], ACT.Copy).then_inc(const_ready, 1)
            act.activation(sel[:, :], const[0:KX, C_SEL:C_SEL + K0], ACT.Copy).then_inc(const_ready, 1)
            act.activation(ident[:, :], const[:, C_ID:C_ID + P], ACT.Copy).then_inc(const_ready, 1)
            act.wait_ge(bias_in, 3 * 16)
            act.mul(bias2d[:, :], bias[:, 2:3], float(D)).then_inc(bias2d_ready, 1)
            for w in range(QPT):
                evacuate_unit(w)
            evacuate_base(0)
            evacuate_x1(0, T0)
            chunk(0, False, True, [QPT, QPT + 1])
            chunk(1, True, True, [QPT + 2])
            with act.Fori(2, FULL) as c:
                chunk(c, True, True, [c + QPT + 1])
            with act.Fori(FULL, CHUNKS - 1) as c:
                chunk(c, True, True, [])
            chunk(CHUNKS - 1, True, False, [])
            evacuate_x2(CHUNKS - 1)
            evacuate_turned(CHUNKS - 1)
            for g in range(GROUPS):
                evacuate_gram(CHUNKS - 1, g)
            act.wait_ge(tail_mm, 1)
            act.wait_ge(bias2d_ready, 1)
            act.activation(z[:, 2, :], acc1[:, :], ACT.Identity, bias=bias2d[:, 0:1]).then_inc(tail_act, 1)
            act.wait_ge(mlp_in, 7 * 16)
            for m, src in enumerate([acc0, misc0, misc1, gps[0]]):
                act.wait_ge(tail_mm, 2 + m)
                act.activation(h1[:, m, :], src[:, :], ACT.Relu, bias=bt1[:, m:m + 1]).then_inc(tail_act, 1)
            for m, src in enumerate([gps[1], spread[0]]):
                act.wait_ge(tail_mm, 6 + m)
                act.activation(h2[:, m, :], src[:, :], ACT.Relu, bias=bt2[:, m:m + 1]).then_inc(tail_act, 1)
            act.wait_ge(tail_mm, 8)
            act.activation(y[:, :], spread[1][0:1, :], ACT.Copy).then_inc(tail_act, 1)


def constants():
    pack = np.zeros((P, C_ALL), np.float32)
    for row in range(KX):
        j = row % F
        pack[row, C_ROT + j:C_ROT + ROTW:F] = 1.0
        pack[row, C_SEL + j:C_SEL + K0:R0] = 1.0
    for row in range(P):
        pack[row, C_MASK + row % GB] = 1.0
        pack[row, C_ID + row] = 1.0
    return pack


def layer0_layout(w):
    w = w.reshape(H, F, F)
    pair = np.zeros((K0, 2, T0, H), np.float32)
    i = np.arange(F)
    for tile in range(T0):
        for u in range(3):
            shift = 3 * tile + u
            if shift > F // 2:
                continue
            pair[R0 * u:R0 * u + F, 0, tile] = w[:, i, (i + shift) % F].T
            if shift:
                pair[R0 * u:R0 * u + F, 1, tile] = w[:, (i + shift) % F, i].T
    return pair.reshape(K0, 2, T0 * H)


def kernel(**inputs):
    import concourse.bacc as bacc
    from concourse.bass_utils import run_bass_kernel_spmd

    def host(name):
        return np.ascontiguousarray(np.asarray(inputs[name]))

    k = np.arange(P)
    w1 = host("L0_rec_W1").reshape(H, F, H)
    arrays = {f"tbl_{f}": host(f"tbl_{f}") for f in range(F)}
    arrays |= {
        "ids": host("ids"),
        "const": constants(),
        "w0ab": layer0_layout(host("L0_rec_W0")),
        "w1": np.stack([w1[:, (k + s) % F, k].T for s in range(F)], axis=1),
        "w2": host("L0_rec_W2").reshape(H, F, H).transpose(2, 1, 0),
        "b0": host("L0_rec_b0"), "b1": host("L0_rec_b1"), "b2": host("L0_rec_b2"),
        "W_top1": host("W_top1"), "W_top2": host("W_top2"),
        "dense_t": host("dense_ctx").T,
        "w_top3": host("W_top3").reshape(HID2 // P, P).T,
        "b_top1": host("b_top1").reshape(HID1 // P, P).T,
        "b_top2": host("b_top2").reshape(HID2 // P, P).T,
    }
    nc = bacc.Bacc("TRN2", target_bir_lowering=False, num_devices=1)
    aps = {}
    for name in arrays:
        arrays[name] = np.ascontiguousarray(arrays[name])
        aps[name] = nc.dram_tensor(f"in_{name}", arrays[name].shape, mybir.dt.from_np(arrays[name].dtype),
                                   kind="ExternalInput").ap()
    aps["out"] = nc.dram_tensor("out_y", (B, 1), F32, kind="ExternalOutput").ap()
    build(nc, aps)
    r = run_bass_kernel_spmd(nc, [{f"in_{n}": v for n, v in arrays.items()}], core_ids=[0])
    return r.results[0]["out_y"]
```

```python
from contextlib import ExitStack

import numpy as np

import concourse.bass as bass
from concourse import mybir

F32 = mybir.dt.float32
I32 = mybir.dt.int32
U32 = mybir.dt.uint32
ALU = mybir.AluOpType
ACT = mybir.ActivationFunctionType
AX = mybir.AxisListType

P = 128
B, F, D, H = 512, 39, 16, 128
FI, FO = 4, -(-F // 4)
FP = FI * FO
CB = P // FI
COLS = CB * D
CHUNKS = B // CB
GB = 8
GROUPS = CB // GB
R0 = F + 1
K0 = 3 * R0
T0 = (F // 2 + 1 + 2) // 3
COPIES = -(-(P + F - 1) // F)
HID1, HID2, DENSE = 512, 256, 16
XT = 4

C_FI, C_B, C_MASK = 0, FI, FI + CB
C_ID = C_MASK + GB
C_ALL = C_ID + P

def steps_with(l0_before):
    steps = []
    for s in range(F):
        if s in l0_before:
            steps.append((0, l0_before.index(s)))
        steps.append((1, s))
    return steps


STEPS_CHUNK0 = steps_with((6, 10, 14, 18, 22, 26, 30))
STEPS_NEXT = steps_with((0, 5, 10, 15, 20, 25, 30))
STEPS_LAST = [(1, s) for s in range(F)]
STEPS_FIRST = [(0, t) for t in range(T0)]
NSTEP = len(STEPS_NEXT)
RING = 10
W2_PART = F // (CHUNKS - 3)
PRODS = 4
assert len(STEPS_CHUNK0) == NSTEP == F + T0
TURN_AFTER, LAY_AFTER, X0T_AFTER, G_AFTER = 2, 12, 18, (8, 15, 21, 26)


def first_step(c):
    return T0 + NSTEP * c


def last_l0(steps):
    return steps.index((0, T0 - 1))


def slot_uses(c, i):
    slot = i % RING
    return (slot < T0) + c * len(range(slot, NSTEP, RING)) + i // RING + 1


def steps_until_free(c, i, ring):
    slot = i % ring
    if i >= ring:
        return first_step(c) + i - ring + 1
    if isinstance(c, int) and c == 0:
        return range(slot, T0, ring)[-1] + 1 if slot < T0 else 0
    return first_step(c - 1) + range(slot, NSTEP, ring)[-1] + 1


def wait_done(engine, semaphore, count):
    if not (isinstance(count, int) and count <= 0):
        engine.wait_ge(semaphore, count)


def build(nc, a):
    ctx = ExitStack()
    with ctx:
        def sb(name, shape, dt=F32):
            return ctx.enter_context(nc.sbuf_tensor(name, shape, dt))

        def ps(name, shape=(P, 512), dt=F32):
            return ctx.enter_context(nc.psum_tensor(name, list(shape), dt))

        def sem(name):
            return ctx.enter_context(nc.semaphore(name))

        const = sb("const", [P, C_ALL])
        rows = sb("rows", [P, CHUNKS, FO], I32)
        first_row = sb("first_row", [P, FO], I32)
        emb = sb("emb", [P, 2, FO * D])
        wide = sb("wide", [P, D, FP])
        x0 = sb("x0", [FP, COLS])
        x0t = sb("x0t", [P, XT, GROUPS * F])
        w0 = sb("w0", [K0, T0, H])
        w0ab = sb("w0ab", [K0, 2, T0 * H])
        w1 = sb("w1", [P, F, H])
        w2 = sb("w2", [P, F, H])
        x0a = sb("x0a", [K0, COLS])
        tiles = sb("tiles", [P, RING, COLS])
        x1 = sb("x1", [P, 2, COLS])
        x2 = sb("x2", [P, COLS])
        x2t = sb("x2t", [P, GROUPS, H])
        diag = sb("diag", [P, GROUPS, GB, F])
        prod = sb("prod", [P, PRODS, COLS])
        gram = sb("gram", [P, F, B])
        z = sb("z", [P, 3, B])
        wt1 = sb("wt1", [P, 3, HID1])
        wt1d = sb("wt1d", [DENSE, HID1])
        dense = sb("dense", [DENSE, B])
        wt2 = sb("wt2", [P, HID1 // P, HID2])
        wt3 = sb("wt3", [P, HID2 // P])
        bias = sb("bias", [P, 3])
        bias2d = sb("bias2d", [P, 1])
        bt1 = sb("bt1", [P, HID1 // P])
        bt2 = sb("bt2", [P, HID2 // P])
        y = sb("y", [1, B])
        h1, h2 = tiles[:, 0:4, :], tiles[:, 4:6, :]
        scratch = nc.dram_tensor("x0_rows", (CHUNKS, COPIES * F, COLS), F32, kind="Internal").ap()

        acc0, acc1 = ps("acc0"), ps("acc1")
        misc0, misc1 = ps("misc0"), ps("misc1")
        gps = [ps("gps0"), ps("gps1")]
        hid_ps = [ps("hid_ps0"), ps("hid_ps1")]

        ids_in, const_in, w0_in, w1_in, w2_in = (sem(n) for n in ("ids_in", "const_in", "w0_in", "w1_in", "w2_in"))
        bias_in, mlp_in, out_done = sem("bias_in"), sem("mlp_in"), sem("out_done")
        gathered = [sem(f"gathered{i}") for i in range(2)]
        tile_in = [sem(f"tile_in{i}") for i in range(RING)]
        bias2d_ready = sem("bias2d_ready")
        w0_ready = sem("w0_ready")
        rows_ready = sem("rows_ready")
        wide_ready = sem("wide_ready")
        lay_done, x0_ready = sem("lay_done"), sem("x0_ready")
        scratch_in = sem("scratch_in")
        x0a_in = sem("x0a_in")
        prod_ready = sem("prod_ready")
        main_done = sem("main_done")
        x1_ready, x2_ready = sem("x1_ready"), sem("x2_ready")
        x0t_done, x0t_ready = sem("x0t_done"), sem("x0t_ready")
        diag_ready = sem("diag_ready")
        x2t_done, x2t_ready = sem("x2t_done"), sem("x2t_ready")
        g_done, g_ready = sem("g_done"), sem("g_ready")
        z_sums = sem("z_sums")
        tail_mm, tail_act = sem("tail_mm"), sem("tail_act")

        def ring(buf, c):
            return buf[:, bass.ds(c & 1, 1), :].rearrange("p c n -> p (c n)")

        def chunk_rows(c):
            return scratch[bass.ds(c, 1), :, :].rearrange("c r n -> (c r) n")

        block = ctx.enter_context(nc.Block())

        @block.sync
        def _(sp):
            def load_x0a(c):
                for u in range(3):
                    sp.dma_start(x0a[u * R0:(u + 1) * R0, :], chunk_rows(c)[0:R0, :]).then_inc(x0a_in, 16)

            def load_tile(layer, k, c, slot):
                m, shift = (P, k) if layer else (K0, 3 * k)
                sp.dma_start(tiles[0:m, slot, :], chunk_rows(c)[shift:shift + m, :]).then_inc(tile_in[slot], 16)

            def chunk(c, steps, nxt):
                for i, (layer, k) in enumerate(steps):
                    if isinstance(c, int) and c == 0 and (layer, k) == (0, 0):
                        sp.wait_ge(scratch_in, 2 * 16)
                        load_x0a(1)
                    wait_done(sp, prod_ready, steps_until_free(c, i, RING))
                    load_tile(layer, k, c if layer else c + 1, i % RING)
                if nxt:
                    ready, free = 16 * (c + 3), first_step(c) + last_l0(steps) + 1
                    if not isinstance(c, int):
                        free = sp.to_reg(free)
                    sp.wait_ge(scratch_in, ready)
                    sp.wait_ge(prod_ready, free)
                    load_x0a(c + 2)

            sp.dma_start(rows[:, :, :], a["ids"]).then_inc(ids_in, 16)
            sp.dma_start(first_row[:, :], a["first_row"]).then_inc(ids_in, 16)
            sp.dma_start(const[:, :], a["const"]).then_inc(const_in, 16)
            sp.dma_start(w0ab[:, :, :], a["w0ab"]).then_inc(w0_in, 16)
            for i in range(3):
                sp.dma_start(bias[:, i:i + 1], a[f"b{i}"].rearrange("(p o) -> p o", o=1)).then_inc(bias_in, 16)
            sp.dma_start(w1[:, :, :], a["w1"]).then_inc(w1_in, 16)
            sp.wait_ge(scratch_in, 16)
            load_x0a(0)
            for i in range(T0):
                load_tile(0, i, 0, i)
            chunk(0, STEPS_CHUNK0, True)
            with sp.Fori(1, CHUNKS - 2) as c:
                sp.dma_start(w2[:, bass.ds((c - 1) * W2_PART, W2_PART), :],
                             a["w2"][:, bass.ds((c - 1) * W2_PART, W2_PART), :]).then_inc(w2_in, 16)
                chunk(c, STEPS_NEXT, True)
            chunk(CHUNKS - 2, STEPS_NEXT, False)
            sp.dma_start(wt1[:, :, :], a["W_top1"][0:3 * H, :].rearrange("(i p) n -> p i n", p=P)).then_inc(mlp_in, 16)
            sp.dma_start(wt1d[:, :], a["W_top1"][3 * H:, :]).then_inc(mlp_in, 16)
            sp.dma_start(dense[:, :], a["dense_t"]).then_inc(mlp_in, 16)
            sp.dma_start(wt2[:, :, :], a["W_top2"].rearrange("(i p) n -> p i n", p=P)).then_inc(mlp_in, 16)
            sp.dma_start(wt3[:, :], a["w_top3"]).then_inc(mlp_in, 16)
            sp.dma_start(bt1[:, :], a["b_top1"]).then_inc(mlp_in, 16)
            sp.dma_start(bt2[:, :], a["b_top2"]).then_inc(mlp_in, 16)
            chunk(CHUNKS - 1, STEPS_LAST, False)
            sp.wait_ge(tail_act, 8)
            sp.dma_start(a["out"].rearrange("b o -> o b"), y[:, :]).then_inc(out_done, 16)
            sp.wait_ge(out_done, 16)

        @block.gpsimd
        def _(pool):
            def gather(c, buf):
                for fo in range(FO):
                    pool.indirect_dma_start(
                        emb[:, buf, fo * D:(fo + 1) * D], None, a["tables"],
                        bass.IndirectOffsetOnAxis(ap=rows[:, c, fo:fo + 1].bitcast(U32), axis=0),
                    ).then_inc(gathered[buf], 16)

            def widen(c, buf):
                pool.wait_ge(gathered[buf], 16 * FO * (c // 2 + 1))
                if c:
                    pool.wait_ge(lay_done, c)
                e = emb[:, buf, :].rearrange("p (f d o) -> p d f o", d=D, o=1).to_broadcast([P, D, FO, FI])
                mask = const[:, C_FI:C_FI + FI].rearrange("p (d f o) -> p d f o", d=1, f=1)
                pool.tensor_tensor(wide[:, :, :].rearrange("p d (f o) -> p d f o", o=FI), e,
                                   mask.to_broadcast([P, D, FO, FI]), ALU.mult).then_inc(wide_ready, 1)

            pool.wait_ge(ids_in, 2 * 16)
            base = first_row[:, :].rearrange("p (o f) -> p o f", o=1).to_broadcast([P, CHUNKS, FO])
            pool.tensor_tensor(rows[:, :, :], rows[:, :, :], base, ALU.add).then_inc(rows_ready, 1)
            pool.wait_ge(rows_ready, 1)
            gather(0, 0)
            pool.wait_ge(const_in, 16)
            for c in range(CHUNKS):
                if c == 0:
                    widen(0, 0)
                if c + 1 < CHUNKS:
                    wait_done(pool, wide_ready, c)
                    gather(c + 1, (c + 1) % 2)
                if c:
                    widen(c, c % 2)

        @block.tensor
        def _(pe):
            def lay_out(c):
                pe.wait_ge(wide_ready, c + 1)
                for d in range(D):
                    mm = pe.matmul(misc1[0:FP, d * CB:(d + 1) * CB], wide[:, d, :], const[:, C_B:C_B + CB],
                                   start=True, stop=True)
                mm.then_inc(lay_done, 1)

            def turn_x0(c):
                pe.wait_ge(x0_ready, c + 1)
                for g in range(GROUPS):
                    mm = pe.matmul(misc1[:, g * F:(g + 1) * F], x0[0:F, g * P:(g + 1) * P],
                                   const[0:F, C_ID:C_ID + F], start=True, stop=True)
                mm.then_inc(x0t_done, 1)

            def turn_x2():
                for g in range(GROUPS):
                    mm = pe.transpose(misc0[:, g * H:(g + 1) * H], x2[:, g * P:(g + 1) * P],
                                      const[:, C_ID:C_ID + P])
                mm.then_inc(x2t_done, 1)

            def contract(layer, k, buf):
                if layer:
                    mm = pe.matmul(acc1[:, :], w1[:, k, :], prod[:, buf, :], start=(k == 0), stop=(k == F - 1))
                else:
                    mm = pe.matmul(acc0[:, :], w0[:, k, :], prod[0:K0, buf, :], start=(k == 0), stop=(k == T0 - 1))
                mm.then_inc(main_done, 1)

            def gram_group(c, g):
                if g == 0:
                    pe.wait_ge(x2t_ready, c + 1)
                    pe.wait_ge(diag_ready, c + 1)
                wait_done(pe, g_ready, GROUPS * c if g < 2 else GROUPS * c + g - 1)
                pe.matmul(gps[g % 2][:, 0:GB * F], x2t[:, g, :],
                          diag[:, g, :, :].rearrange("p b j -> p (b j)"), start=True, stop=True).then_inc(g_done, 1)

            def chunk(c, steps, prev, lay):
                for i, (layer, k) in enumerate(steps):
                    pe.wait_ge(prod_ready, first_step(c) + i + 1)
                    if layer and k == 0 and prev:
                        pe.wait_ge(x2_ready, c)
                    if not layer and k == 0:
                        pe.wait_ge(x1_ready, c + 1)
                    contract(layer, k, i % PRODS)
                    if not layer:
                        continue
                    if prev and k == TURN_AFTER:
                        pe.wait_ge(x2_ready, c)
                        wait_done(pe, x2t_ready, c - 1)
                        turn_x2()
                    if k == 1 and not prev:
                        pe.wait_ge(x0t_ready, 1)
                        lay_out(1)
                        turn_x0(1)
                    if lay and k == LAY_AFTER:
                        pe.wait_ge(x0t_ready, c + 2)
                        lay_out(c + 2)
                    if lay and k == X0T_AFTER:
                        turn_x0(c + 2)
                    if prev and k in G_AFTER:
                        gram_group(c - 1, G_AFTER.index(k))

            pe.wait_ge(const_in, 16)
            lay_out(0)
            turn_x0(0)
            pe.wait_ge(w0_ready, 1)
            for i in range(T0):
                pe.wait_ge(prod_ready, i + 1)
                contract(0, i, i % PRODS)
            pe.wait_ge(w1_in, 16)
            chunk(0, STEPS_CHUNK0, False, True)
            chunk(1, STEPS_NEXT, True, True)
            with pe.Fori(2, CHUNKS - 2) as c:
                chunk(c, STEPS_NEXT, True, True)
            chunk(CHUNKS - 2, STEPS_NEXT, True, False)
            chunk(CHUNKS - 1, STEPS_LAST, True, False)

            pe.wait_ge(x2_ready, CHUNKS)
            turn_x2()
            for g in range(GROUPS):
                gram_group(CHUNKS - 1, g)
            pe.wait_ge(w2_in, 16 * (F // W2_PART))
            pe.wait_ge(g_ready, GROUPS * CHUNKS)
            for j in range(F):
                mm = pe.matmul(acc1[:, :], w2[:, j, :], gram[:, j, :], start=(j == 0), stop=(j == F - 1))
            mm.then_inc(tail_mm, 1)
            pe.wait_ge(mlp_in, 7 * 16)
            pe.wait_ge(z_sums, 2 * CHUNKS)
            hid = [acc0, misc0, misc1, gps[0]]
            for m in range(HID1 // P):
                cols = slice(m * P, (m + 1) * P)
                pe.matmul(hid[m][:, :], wt1[:, 0, cols], z[:, 0, :], start=True, stop=False)
                pe.matmul(hid[m][:, :], wt1[:, 1, cols], z[:, 1, :], start=False, stop=False)
                pe.matmul(hid[m][:, :], wt1d[:, cols], dense[:, :], start=False, stop=False)
            pe.wait_ge(tail_act, 1)
            for m in range(HID1 // P):
                cols = slice(m * P, (m + 1) * P)
                pe.matmul(hid[m][:, :], wt1[:, 2, cols], z[:, 2, :], start=False, stop=True).then_inc(tail_mm, 1)
            hid2 = hid_ps
            for i in range(HID1 // P):
                pe.wait_ge(tail_act, 2 + i)
                for m in range(HID2 // P):
                    mm = pe.matmul(hid2[m][:, :], wt2[:, i, m * P:(m + 1) * P], h1[:, i, :],
                                   start=(i == 0), stop=(i == HID1 // P - 1))
                    if i == HID1 // P - 1:
                        mm.then_inc(tail_mm, 1)
            for i in range(HID2 // P):
                pe.wait_ge(tail_act, 6 + i)
                mm = pe.matmul(acc1[0:1, :], wt3[:, i:i + 1], h2[:, i, :],
                               start=(i == 0), stop=(i == HID2 // P - 1))
            mm.then_inc(tail_mm, 1)

        @block.vector
        def _(dve):
            def multiply(layer, c, slot, buf):
                m = P if layer else K0
                other = ring(x1, c) if layer else x0a[:, :]
                dve.tensor_tensor(prod[0:m, buf, :], tiles[0:m, slot, :], other, ALU.mult).then_inc(prod_ready, 1)

            def sum_dims(layer, c, src):
                dve.tensor_reduce(z[:, layer, bass.ds(c * CB, CB)].rearrange("p (g b) -> p g b", g=GROUPS),
                                  src.rearrange("p (g d b) -> p g b d", g=GROUPS, d=D), AX.X,
                                  ALU.add).then_inc(z_sums, 1)

            def block_diagonal(c):
                dve.wait_ge(x0t_ready, c + 1)
                wait_done(dve, g_done, GROUPS * c)
                turned = x0t[:, bass.ds(c & (XT - 1), 1), :].rearrange("p c (g o j) -> p (c g) o j", g=GROUPS, o=1)
                mask = const[:, C_MASK:C_MASK + GB].rearrange("p (g b o) -> p g b o", g=1, o=1)
                dve.tensor_tensor(diag[:, :, :, :], turned.to_broadcast([P, GROUPS, GB, F]),
                                  mask.to_broadcast([P, GROUPS, GB, F]), ALU.mult).then_inc(diag_ready, 1)

            def chunk(c, steps, prev):
                for i, (layer, k) in enumerate(steps):
                    if layer and k == 0:
                        dve.wait_ge(x1_ready, c + 1)
                    if not layer and k == 0:
                        dve.wait_ge(x0a_in, 3 * 16 * (c + 2))
                    dve.wait_ge(tile_in[i % RING], 16 * slot_uses(c, i))
                    dve.wait_ge(main_done, steps_until_free(c, i, PRODS))
                    multiply(layer, c, i % RING, i % PRODS)
                    if layer and k == 2 and prev:
                        block_diagonal(c - 1)
                    if layer and k == 3 and prev:
                        dve.wait_ge(x2_ready, c)
                        sum_dims(1, c - 1, x2[:, :])
                    if layer and k == 5:
                        sum_dims(0, c, ring(x1, c))

            dve.wait_ge(w0_in, 16)
            dve.tensor_tensor(w0[:, :, :].rearrange("p s h -> p (s h)"), w0ab[:, 0], w0ab[:, 1],
                              ALU.add).then_inc(w0_ready, 1)
            dve.wait_ge(const_in, 16)
            dve.wait_ge(x0a_in, 3 * 16)
            for i in range(T0):
                dve.wait_ge(tile_in[i], 16)
                wait_done(dve, main_done, i - PRODS + 1)
                multiply(0, -1, i, i % PRODS)
            chunk(0, STEPS_CHUNK0, False)
            chunk(1, STEPS_NEXT, True)
            with dve.Fori(2, CHUNKS - 1) as c:
                chunk(c, STEPS_NEXT, True)
            chunk(CHUNKS - 1, STEPS_LAST, True)
            block_diagonal(CHUNKS - 1)
            dve.wait_ge(x2_ready, CHUNKS)
            sum_dims(1, CHUNKS - 1, x2[:, :])

        @block.scalar
        def _(act):
            def evacuate_layout(c):
                act.wait_ge(lay_done, c + 1)
                if isinstance(c, int) and c == 0:
                    pass
                else:
                    act.wait_ge(x0t_done, c)
                    act.wait_ge(scratch_in, 16 * c)
                act.activation(x0[:, :].rearrange("p (g d b) -> p g d b", g=GROUPS, d=D),
                               misc1[0:FP, :].rearrange("p (d g b) -> p g d b", d=D, b=GB),
                               ACT.Copy).then_inc(x0_ready, 1)
                act.wait_ge(x0_ready, c + 1)
                act.dma_start(chunk_rows(c).rearrange("(u j) n -> j u n", u=COPIES),
                              x0[0:F, :].rearrange("p (u n) -> p u n", u=1).to_broadcast([F, COPIES, COLS]),
                              ).then_inc(scratch_in, 16)

            def evacuate_x0t(c):
                act.wait_ge(x0t_done, c + 1)
                act.activation(x0t[:, bass.ds(c & (XT - 1), 1), :].rearrange("p c n -> p (c n)"),
                               misc1[:, 0:GROUPS * F], ACT.Copy).then_inc(x0t_ready, 1)

            def evacuate_x1(c, steps_done):
                act.wait_ge(main_done, steps_done)
                act.activation(ring(x1, c), acc0[:, :], ACT.Identity,
                               bias=bias[:, 0:1]).then_inc(x1_ready, 1)

            def evacuate_x2(c):
                act.wait_ge(main_done, first_step(c + 1) if not isinstance(c, int) or c < CHUNKS - 1
                            else first_step(c) + len(STEPS_LAST))
                wait_done(act, x2t_done, c)
                wait_done(act, z_sums, 2 * c)
                act.activation(x2[:, :], acc1[:, :], ACT.Identity, bias=bias[:, 1:2]).then_inc(x2_ready, 1)

            def evacuate_x2t(c):
                act.wait_ge(x2t_done, c + 1)
                act.activation(x2t[:, :, :].rearrange("p g h -> p (g h)"), misc0[:, :],
                               ACT.Copy).then_inc(x2t_ready, 1)

            def evacuate_gram(c, g):
                act.wait_ge(g_done, GROUPS * c + g + 1)
                act.activation(gram[:, :, bass.ds(c * CB + g * GB, GB)],
                               gps[g % 2][:, 0:GB * F].rearrange("p (b j) -> p j b", b=GB),
                               ACT.Copy).then_inc(g_ready, 1)

            def chunk(c, prev, nxt, lay):
                if prev:
                    evacuate_x2(c - 1)
                    evacuate_x2t(c - 1)
                    evacuate_gram(c - 1, 0)
                if lay:
                    evacuate_layout(c + 2)
                if prev:
                    evacuate_gram(c - 1, 1)
                if lay:
                    evacuate_x0t(c + 2)
                if prev:
                    evacuate_gram(c - 1, 2)
                    evacuate_gram(c - 1, 3)
                if nxt:
                    evacuate_x1(c + 1, first_step(c) + last_l0(STEPS_NEXT if prev else STEPS_CHUNK0) + 1)

            act.wait_ge(bias_in, 3 * 16)
            act.mul(bias2d[:, :], bias[:, 2:3], float(D)).then_inc(bias2d_ready, 1)
            evacuate_layout(0)
            evacuate_x0t(0)
            evacuate_x1(0, T0)
            evacuate_layout(1)
            evacuate_x0t(1)
            chunk(0, False, True, True)
            chunk(1, True, True, True)
            with act.Fori(2, CHUNKS - 2) as c:
                chunk(c, True, True, True)
            chunk(CHUNKS - 2, True, True, False)
            chunk(CHUNKS - 1, True, False, False)
            evacuate_x2(CHUNKS - 1)
            evacuate_x2t(CHUNKS - 1)
            for g in range(GROUPS):
                evacuate_gram(CHUNKS - 1, g)
            act.wait_ge(tail_mm, 1)
            act.wait_ge(bias2d_ready, 1)
            act.activation(z[:, 2, :], acc1[:, :], ACT.Identity, bias=bias2d[:, 0:1]).then_inc(tail_act, 1)
            act.wait_ge(mlp_in, 7 * 16)
            for m, src in enumerate([acc0, misc0, misc1, gps[0]]):
                act.wait_ge(tail_mm, 2 + m)
                act.activation(h1[:, m, :], src[:, :], ACT.Relu, bias=bt1[:, m:m + 1]).then_inc(tail_act, 1)
            for m, src in enumerate(hid_ps):
                act.wait_ge(tail_mm, 6 + m)
                act.activation(h2[:, m, :], src[:, :], ACT.Relu, bias=bt2[:, m:m + 1]).then_inc(tail_act, 1)
            act.wait_ge(tail_mm, 8)
            act.activation(y[:, :], acc1[0:1, :], ACT.Copy).then_inc(tail_act, 1)


def constants():
    pack = np.zeros((P, C_ALL), np.float32)
    for row in range(P):
        pack[row, C_FI + row // CB] = 1.0
        pack[row, C_B + row % CB] = 1.0
        pack[row, C_MASK + row % GB] = 1.0
        pack[row, C_ID + row] = 1.0
    return pack


def layer0_layout(w):
    w = w.reshape(H, F, F)
    pair = np.zeros((K0, 2, T0, H), np.float32)
    i = np.arange(F)
    for tile in range(T0):
        for u in range(3):
            shift = 3 * tile + u
            if shift > F // 2:
                continue
            pair[R0 * u:R0 * u + F, 0, tile] = w[:, i, (i + shift) % F].T
            if shift:
                pair[R0 * u:R0 * u + F, 1, tile] = w[:, (i + shift) % F, i].T
    return pair.reshape(K0, 2, T0 * H)


def kernel(**inputs):
    import concourse.bacc as bacc
    from concourse.bass_utils import run_bass_kernel_spmd

    def host(name):
        return np.ascontiguousarray(np.asarray(inputs[name]))

    k = np.arange(P)
    w1 = host("L0_rec_W1").reshape(H, F, H)
    tables = [host(f"tbl_{f}") for f in range(F)]
    starts = np.cumsum([0] + [len(t) for t in tables])
    field = np.minimum(np.arange(FP), F - 1).reshape(FO, FI)
    arrays = {
        "tables": np.concatenate(tables),
        "ids": host("ids").reshape(CHUNKS, CB, F)[:, :, field].transpose(3, 1, 0, 2).reshape(P, CHUNKS, FO),
        "first_row": np.repeat(starts[field.T].astype(np.int32), CB, axis=0),
        "const": constants(),
        "w0ab": layer0_layout(host("L0_rec_W0")),
        "w1": np.stack([w1[:, (k + s) % F, k].T for s in range(F)], axis=1),
        "w2": host("L0_rec_W2").reshape(H, F, H).transpose(2, 1, 0),
        "b0": host("L0_rec_b0"), "b1": host("L0_rec_b1"), "b2": host("L0_rec_b2"),
        "W_top1": host("W_top1"), "W_top2": host("W_top2"),
        "dense_t": host("dense_ctx").T,
        "w_top3": host("W_top3").reshape(HID2 // P, P).T,
        "b_top1": host("b_top1").reshape(HID1 // P, P).T,
        "b_top2": host("b_top2").reshape(HID2 // P, P).T,
    }
    nc = bacc.Bacc("TRN2", target_bir_lowering=False, num_devices=1)
    aps = {}
    for name in arrays:
        arrays[name] = np.ascontiguousarray(arrays[name])
        aps[name] = nc.dram_tensor(f"in_{name}", arrays[name].shape, mybir.dt.from_np(arrays[name].dtype),
                                   kind="ExternalInput").ap()
    aps["out"] = nc.dram_tensor("out_y", (B, 1), F32, kind="ExternalOutput").ap()
    build(nc, aps)
    r = run_bass_kernel_spmd(nc, [{f"in_{n}": v for n, v in arrays.items()}], core_ids=[0])
    return r.results[0]["out_y"]
```

```python
from contextlib import ExitStack

import numpy as np

import concourse.bass as bass
from concourse import mybir

F32 = mybir.dt.float32
F32R = mybir.dt.float32r
I32 = mybir.dt.int32
U32 = mybir.dt.uint32
ALU = mybir.AluOpType
ACT = mybir.ActivationFunctionType
AX = mybir.AxisListType

P = 128
B, F, D, H = 512, 39, 16, 128
FI, FO = 4, -(-F // 4)
FP = FI * FO
F1 = F + 1
CB = P // FI
COLS = CB * D
CHUNKS = B // CB
GB = P // D
GROUPS = CB // GB
R0 = F + 1
K0 = 3 * R0
T0 = (F // 2 + 1 + 2) // 3
COPIES = -(-(2 * R0 + F + 3 * T0) // F)
HID1, HID2, DENSE = 512, 256, 16
XT = 4
W1_PARTS = 3

C_FI, C_B, C_MASK = 0, FI, FI + CB
C_ID = C_MASK + GB
C_ALL = C_ID + P

JB = 4
OWNERS = "ADADAADADA"
BLOCKS = len(OWNERS)
HALF = BLOCKS // 2
NA, ND = OWNERS.count("A"), OWNERS.count("D")
NA0, ND0 = OWNERS[:HALF].count("A"), OWNERS[:HALF].count("D")
YA, YD = 4, 2
assert NA * GROUPS % YA == 0 and ND * GROUPS % YD == 0 and JB * BLOCKS >= F > JB * (BLOCKS - 1)
S_BIAS = JB * HALF
S_HALF = S_BIAS + 1
S_SUM = S_HALF + F - JB * HALF
SLOTS = S_SUM + 1
L0_TILES, L0_PRODS = 4, 2

L0_AFTER = ((0, 3), (0, 8), (1, 3), (1, 8), (2, 3), (2, 8), (3, 1))
L0_AFTER_0 = ((1, 3), (1, 6), (1, 9), (2, 2), (2, 5), (2, 8), (3, 1))
LAY_AFTER, X0T_AFTER, G_AFTER = (0, 1), (1, 1), 6
DIAG_AFTER = {0: 0, 2: 1, 4: 2, 6: 3}


def fields_of(q):
    return range(JB * q, min(JB * q + JB, F))


def slot_of(q):
    return JB * q if q < HALF else S_HALF + JB * (q - HALF)


def uses_before(i, ring, x):
    if i >= ring:
        return T0 * x + i - ring + 1
    return 0 if isinstance(x, int) and x == 0 else T0 * (x - 1) + range(i, T0, ring)[-1] + 1


def wait_done(engine, semaphore, count):
    if not (isinstance(count, int) and count <= 0):
        engine.wait_ge(semaphore, count)


def build(nc, a):
    ctx = ExitStack()
    with ctx:
        def sb(name, shape, dt=F32):
            return ctx.enter_context(nc.sbuf_tensor(name, shape, dt))

        def ps(name, shape=(P, 512), dt=F32):
            return ctx.enter_context(nc.psum_tensor(name, list(shape), dt))

        def sem(name):
            return ctx.enter_context(nc.semaphore(name))

        const = sb("const", [P, C_ALL])
        rows = sb("rows", [P, CHUNKS, FO], I32)
        first_row = sb("first_row", [P, FO], I32)
        emb = sb("emb", [P, 2, FO * D])
        wide = sb("wide", [P, D, FP])
        x0 = sb("x0", [FP, COLS])
        x0t = sb("x0t", [P, XT, GROUPS * F1])
        w0 = sb("w0", [K0, T0, H])
        w1h = sb("w1h", [P, F * H], F32R)
        w1l = sb("w1l", [P, F * H], F32R)
        w2 = sb("w2", [P, F, H])
        x0a = sb("x0a", [K0, COLS])
        tiles = sb("tiles", [K0, L0_TILES, COLS])
        prod0 = sb("prod0", [K0, L0_PRODS, COLS])
        x1 = sb("x1", [P, COLS])
        x1h = sb("x1h", [P, COLS], F32R)
        x1l = sb("x1l", [P, COLS], F32R)
        prods = sb("prods", [P, SLOTS, H])
        x2t = sb("x2t", [P, GROUPS, H])
        diag = sb("diag", [P, 2, GB, F1])
        gram = sb("gram", [P, F1, B])
        z = sb("z", [P, 2, B])
        wt3 = sb("wt3", [P, HID2 // P])
        bias = sb("bias", [P, 2])
        bias2d = sb("bias2d", [P, 1])
        bt1 = sb("bt1", [P, HID1 // P])
        bt2 = sb("bt2", [P, HID2 // P])
        y = sb("y", [1, B])
        w0ab = gram[0:K0, 0:4, :].rearrange("p j b -> p (j b)")[:, 0:2 * T0 * H].rearrange("p (i n) -> p i n", i=2)
        after = prods[:, :, :].rearrange("p s h -> p (s h)")
        wt1 = after[:, 0:2 * HID1].rearrange("p (i n) -> p i n", i=2)
        wt2 = after[:, 2 * HID1:2 * HID1 + HID1 // P * HID2].rearrange("p (i n) -> p i n", i=HID1 // P)
        wt1_0, wt1d, dense = x1[:, :], x0a[0:DENSE, :], tiles[0:DENSE, 0, :]
        h1, h2 = gram[:, 0:4, :], gram[:, 4:6, :]
        scratch = nc.dram_tensor("x0_rows", (CHUNKS, COPIES * F, COLS), F32, kind="Internal").ap()

        acc0, misc = ps("acc0"), ps("misc")
        ya = [ps(f"ya{i}") for i in range(YA)]
        yd = [ps(f"yd{i}") for i in range(YD)]

        ids_in, const_in, w0_in, w1_in, w2_in = (sem(n) for n in ("ids_in", "const_in", "w0_in", "w1_in", "w2_in"))
        bias_in, mlp0_in, mlp_in, out_done = sem("bias_in"), sem("mlp0_in"), sem("mlp_in"), sem("out_done")
        gathered = [sem(f"gathered{i}") for i in range(2)]
        tile_in = [sem(f"tile_in{i}") for i in range(L0_TILES)]
        bias2d_ready = sem("bias2d_ready")
        w0_ready = sem("w0_ready")
        w1h_ready, w1_split = sem("w1h_ready"), sem("w1_split")
        rows_ready = sem("rows_ready")
        ones_ready = sem("ones_ready")
        wide_ready = sem("wide_ready")
        lay_done, x0_ready = sem("lay_done"), sem("x0_ready")
        scratch_in = sem("scratch_in")
        x0a_in = sem("x0a_in")
        prod0_ready, l0_done = sem("prod0_ready"), sem("l0_done")
        x1_ready = sem("x1_ready")
        x1h_front, x1h_back = sem("x1h_front"), sem("x1h_back")
        x1_front, x1_back = sem("x1_front"), sem("x1_back")
        z_sums = sem("z_sums")
        ya_ready, yd_ready = sem("ya_ready"), sem("yd_ready")
        ya_used, yd_used = sem("ya_used"), sem("yd_used")
        sums_done = sem("sums_done")
        x0t_done, x0t_ready = sem("x0t_done"), sem("x0t_ready")
        diag_ready = sem("diag_ready")
        g_done, g_ready = sem("g_done"), sem("g_ready")
        tail_mm, tail_act = sem("tail_mm"), sem("tail_act")

        FRONT, BACK = slice(0, (GROUPS - 1) * P), slice((GROUPS - 1) * P, COLS)

        def chunk_rows(c):
            return scratch[bass.ds(c, 1), :, :].rearrange("c r n -> (c r) n")

        def turned(c):
            return x0t[:, bass.ds(c & (XT - 1), 1), :].rearrange("p c n -> p (c n)")

        def w1_part(i):
            return slice(i * F // W1_PARTS * H, (i + 1) * F // W1_PARTS * H)

        def multiply0(engine, x, i):
            if i == 0:
                engine.wait_ge(x0a_in, 3 * 16 * (x + 1))
            slot = i % L0_TILES
            engine.wait_ge(tile_in[slot], 16 * (x * len(range(slot, T0, L0_TILES)) + i // L0_TILES + 1))
            wait_done(engine, l0_done, uses_before(i, L0_PRODS, x))
            engine.tensor_tensor(prod0[:, i % L0_PRODS, :], tiles[:, slot, :], x0a[:, :],
                                 ALU.mult).then_inc(prod0_ready, 1)

        hid, hid2 = (acc0, ya[0], ya[1], misc), (yd[1], ya[2])
        block = ctx.enter_context(nc.Block())

        @block.sync
        def _(sp):
            def load_layer0(x):
                ready, free = 16 * (x + 1), T0 * x
                if not isinstance(x, int):
                    free = sp.to_reg(free)
                sp.wait_ge(scratch_in, ready)
                wait_done(sp, prod0_ready, free)
                for u in range(3):
                    sp.dma_start(x0a[u * R0:(u + 1) * R0, :], chunk_rows(x)[0:R0, :]).then_inc(x0a_in, 16)
                for i in range(T0):
                    wait_done(sp, prod0_ready, uses_before(i, L0_TILES, x))
                    sp.dma_start(tiles[:, i % L0_TILES, :],
                                 chunk_rows(x)[3 * i:3 * i + K0, :]).then_inc(tile_in[i % L0_TILES], 16)

            sp.dma_start(rows[:, :, :], a["ids"]).then_inc(ids_in, 16)
            sp.dma_start(first_row[:, :], a["first_row"]).then_inc(ids_in, 16)
            sp.dma_start(const[:, :], a["const"]).then_inc(const_in, 16)
            sp.dma_start(w0ab, a["w0ab"]).then_inc(w0_in, 16)
            for i, name in enumerate(("b0", "b2")):
                sp.dma_start(bias[:, i:i + 1], a[name].rearrange("(p o) -> p o", o=1)).then_inc(bias_in, 16)
            sp.dma_start(prods[:, S_BIAS, :], a["b1"].rearrange("(o h) -> o h", o=1).to_broadcast([P, H])
                         ).then_inc(bias_in, 16)
            sp.dma_start(w2[:, :, :], a["w1"]).then_inc(w1_in, 16)
            load_layer0(0)
            load_layer0(1)
            sp.wait_ge(w1_split, W1_PARTS)
            sp.dma_start(w2[:, :, :], a["w2"]).then_inc(w2_in, 16)
            with sp.Fori(2, CHUNKS) as x:
                load_layer0(x)
            sp.dma_start(wt3[:, :], a["w_top3"]).then_inc(mlp_in, 16)
            sp.dma_start(bt1[:, :], a["b_top1"]).then_inc(mlp_in, 16)
            sp.dma_start(bt2[:, :], a["b_top2"]).then_inc(mlp_in, 16)
            sp.wait_ge(prod0_ready, T0 * CHUNKS)
            sp.dma_start(wt1d, a["W_top1"][3 * H:, :]).then_inc(mlp0_in, 16)
            sp.dma_start(dense, a["dense_t"]).then_inc(mlp0_in, 16)
            sp.wait_ge(x1_back, CHUNKS)
            sp.wait_ge(z_sums, CHUNKS)
            sp.dma_start(wt1_0, a["W_top1"][0:H, :]).then_inc(mlp0_in, 16)
            sp.wait_ge(sums_done, 2 * GROUPS * CHUNKS)
            sp.dma_start(wt1, a["W_top1"][H:3 * H, :].rearrange("(i p) n -> p i n", p=P)).then_inc(mlp_in, 16)
            sp.dma_start(wt2, a["W_top2"].rearrange("(i p) n -> p i n", p=P)).then_inc(mlp_in, 16)
            sp.wait_ge(tail_act, 8)
            sp.dma_start(a["out"].rearrange("b o -> o b"), y[:, :]).then_inc(out_done, 16)
            sp.wait_ge(out_done, 16)

        @block.gpsimd
        def _(pool):
            def gather(c, fo_range):
                wait_done(pool, wide_ready, c - 1)
                for fo in fo_range:
                    pool.indirect_dma_start(
                        emb[:, c % 2, fo * D:(fo + 1) * D], None, a["tables"],
                        bass.IndirectOffsetOnAxis(ap=rows[:, c, fo:fo + 1].bitcast(U32), axis=0),
                    ).then_inc(gathered[c % 2], 16)

            def widen(c):
                pool.wait_ge(gathered[c % 2], 16 * FO * (c // 2 + 1))
                if c:
                    pool.wait_ge(lay_done, c)
                e = emb[:, c % 2, :].rearrange("p (f d o) -> p d f o", d=D, o=1).to_broadcast([P, D, FO, FI])
                mask = const[:, C_FI:C_FI + FI].rearrange("p (d f o) -> p d f o", d=1, f=1)
                pool.tensor_tensor(wide[:, :, :].rearrange("p d (f o) -> p d f o", o=FI), e,
                                   mask.to_broadcast([P, D, FO, FI]), ALU.mult).then_inc(wide_ready, 1)

            def block_diagonal(c, g):
                n = GROUPS * c + g
                pool.wait_ge(x0t_ready, c + 1)
                wait_done(pool, g_done, n - 1)
                row = x0t[:, c % XT, g * F1:(g + 1) * F1].rearrange("p (o j) -> p o j", o=1)
                mask = const[:, C_MASK:C_MASK + GB].rearrange("p (b o) -> p b o", o=1)
                pool.tensor_tensor(diag[:, n % 2, :, :], row.to_broadcast([P, GB, F1]),
                                   mask.to_broadcast([P, GB, F1]), ALU.mult).then_inc(diag_ready, 1)

            pool.wait_ge(ids_in, 2 * 16)
            base = first_row[:, :].rearrange("p (o f) -> p o f", o=1).to_broadcast([P, CHUNKS, FO])
            pool.tensor_tensor(rows[:, :, :], rows[:, :, :], base, ALU.add).then_inc(rows_ready, 1)
            pool.wait_ge(rows_ready, 1)
            gather(0, range(FO))
            gather(1, range(3))
            pool.memset(x0t[:, :, :].rearrange("p c (g j) -> p (c g) j", j=F1)[:, :, F:F1], 1.0).then_inc(ones_ready, 1)
            pool.wait_ge(const_in, 16)
            pool.wait_ge(ones_ready, 1)
            widen(0)
            gather(1, range(3, FO))
            gather(2, range(2))
            widen(1)
            gather(2, range(2, FO))
            for c in range(CHUNKS):
                if c + 2 < CHUNKS:
                    widen(c + 2)
                for i in range(T0):
                    if c + 1 < CHUNKS:
                        multiply0(pool, c + 1, i)
                    if i in DIAG_AFTER:
                        block_diagonal(c, DIAG_AFTER[i])
                    if c + 3 < CHUNKS and 2 * i < FO:
                        gather(c + 3, range(2 * i, 2 * i + 2))

        @block.tensor
        def _(pe):
            def lay_out(c):
                pe.wait_ge(wide_ready, c + 1)
                for d in range(D):
                    mm = pe.matmul(misc[0:FP, d * CB:(d + 1) * CB], wide[:, d, :], const[:, C_B:C_B + CB],
                                   start=True, stop=True)
                mm.then_inc(lay_done, 1)

            def turn_x0(c):
                for g in range(GROUPS):
                    mm = pe.transpose(misc[:, g * F:(g + 1) * F], x0[0:F, g * P:(g + 1) * P],
                                      const[0:F, C_ID:C_ID + F])
                mm.then_inc(x0t_done, 1)

            def layer0(x, i):
                pe.wait_ge(prod0_ready, T0 * x + i + 1)
                if i == 0:
                    wait_done(pe, x1_ready, x)
                pe.matmul(acc0[:, :], w0[:, i, :], prod0[:, i % L0_PRODS, :],
                          start=(i == 0), stop=(i == T0 - 1)).then_inc(l0_done, 1)

            def gram_group(n, g):
                pe.wait_ge(sums_done, 2 * n + 2)
                pe.wait_ge(diag_ready, n + 1)
                wait_done(pe, g_ready, n)
                pe.matmul(misc[:, 0:GB * F1], x2t[:, g, :],
                          diag[:, g % 2, :, :].rearrange("p b j -> p (b j)"),
                          start=True, stop=True).then_inc(g_done, 1)

            def layer1_block(n, g, q):
                k = OWNERS[:q].count(OWNERS[q])
                if OWNERS[q] == "A":
                    out, ready = ya[(NA * g + k) % YA], ya_ready
                    wait_done(pe, ya_used, NA * n + k - YA + 1)
                else:
                    out, ready = yd[(ND * g + k) % YD], yd_ready
                    wait_done(pe, yd_used, ND * n + k - YD + 1)
                fields = fields_of(q)
                cols = slice(fields[0] * H, (fields[-1] + 1) * H)
                xs, out = slice(g * P, (g + 1) * P), out[:, 0:len(fields) * H]
                pe.matmul(out, x1h[:, xs], w1h[:, cols], start=True, stop=False)
                pe.matmul(out, x1h[:, xs], w1l[:, cols], start=False, stop=False)
                pe.matmul(out, x1l[:, xs], w1h[:, cols], start=False, stop=True).then_inc(ready, 1)

            def chunk(c, prev, nxt, lay):
                l0_after = L0_AFTER if prev else L0_AFTER_0
                for g in range(GROUPS):
                    if g == 0:
                        pe.wait_ge(x1_front, c + 1)
                    if g == GROUPS - 1:
                        pe.wait_ge(x1_back, c + 1)
                    for q in range(BLOCKS):
                        if lay and (g, q) == X0T_AFTER:
                            pe.wait_ge(x0_ready, c + 3)
                            wait_done(pe, g_ready, GROUPS * c)
                        layer1_block(GROUPS * c + g, g, q)
                        if nxt and (g, q) in l0_after:
                            layer0(c + 1, l0_after.index((g, q)))
                        if lay and (g, q) == LAY_AFTER:
                            pe.wait_ge(x0t_ready, c + 2)
                            wait_done(pe, g_ready, GROUPS * c - 1)
                            lay_out(c + 2)
                        if lay and (g, q) == X0T_AFTER:
                            turn_x0(c + 2)
                        if q == G_AFTER and (g or prev):
                            if lay and g < 2:
                                pe.wait_ge((x0_ready, x0t_ready)[g], c + 3)
                            gram_group(GROUPS * c + g - 1, (g - 1) % GROUPS)

            pe.wait_ge(const_in, 16)
            lay_out(0)
            pe.wait_ge(x0_ready, 1)
            turn_x0(0)
            pe.wait_ge(w0_ready, 1)
            for i in range(T0):
                layer0(0, i)
            pe.wait_ge(x0t_ready, 1)
            lay_out(1)
            pe.wait_ge(x0_ready, 2)
            turn_x0(1)
            pe.wait_ge(w1_split, W1_PARTS)
            chunk(0, False, True, True)
            with pe.Fori(1, CHUNKS - 2) as c:
                chunk(c, True, True, True)
            chunk(CHUNKS - 2, True, True, False)
            chunk(CHUNKS - 1, True, False, False)

            def hidden1_early(m):
                cols = slice(m * P, (m + 1) * P)
                pe.matmul(hid[m][:, :], wt1_0[:, cols], z[:, 0, :], start=True, stop=False)
                pe.matmul(hid[m][:, :], wt1d[:, cols], dense, start=False, stop=False)

            pe.wait_ge(mlp0_in, 3 * 16)
            pe.wait_ge(z_sums, CHUNKS)
            hidden1_early(0)
            pe.wait_ge(ya_used, NA * GROUPS * CHUNKS - 2)
            hidden1_early(1)
            hidden1_early(2)
            gram_group(GROUPS * CHUNKS - 1, GROUPS - 1)

            l2 = yd[0]
            pe.wait_ge(w2_in, 16)
            pe.wait_ge(g_ready, GROUPS * CHUNKS)
            for j in range(F):
                mm = pe.matmul(l2[:, :], w2[:, j, :], gram[:, j, :], start=(j == 0), stop=(j == F - 1))
            mm.then_inc(tail_mm, 1)
            hidden1_early(3)
            pe.wait_ge(mlp_in, 5 * 16)
            for m, out in enumerate(hid):
                pe.matmul(out[:, :], wt1[:, 0, m * P:(m + 1) * P], gram[:, F, :], start=False, stop=False)
            pe.wait_ge(tail_act, 1)
            for m, out in enumerate(hid):
                pe.matmul(out[:, :], wt1[:, 1, m * P:(m + 1) * P], z[:, 1, :],
                          start=False, stop=True).then_inc(tail_mm, 1)
            for i in range(HID1 // P):
                pe.wait_ge(tail_act, 2 + i)
                for m, out in enumerate(hid2):
                    mm = pe.matmul(out[:, :], wt2[:, i, m * P:(m + 1) * P], h1[:, i, :],
                                   start=(i == 0), stop=(i == HID1 // P - 1))
                    if i == HID1 // P - 1:
                        mm.then_inc(tail_mm, 1)
            for i in range(HID2 // P):
                pe.wait_ge(tail_act, 6 + i)
                mm = pe.matmul(l2[0:1, :], wt3[:, i:i + 1], h2[:, i, :],
                               start=(i == 0), stop=(i == HID2 // P - 1))
            mm.then_inc(tail_mm, 1)

        @block.vector
        def _(dve):
            def multiply(c, g, q):
                n, k, fields = GROUPS * c + g, OWNERS[:q].count("D"), fields_of(q)
                w, slot, at = len(fields), slot_of(q), g * F1 + fields[0]
                dve.wait_ge(yd_ready, ND * n + k + 1)
                if k in (0, ND0):
                    wait_done(dve, sums_done, 2 * n + (1 if k else 0) - 1)
                dve.tensor_tensor(prods[:, slot:slot + w, :],
                                  yd[(ND * g + k) % YD][:, 0:w * H].rearrange("p (j h) -> p j h", h=H),
                                  turned(c)[:, at:at + w].rearrange("p (j o) -> p j o", o=1).to_broadcast([P, w, H]),
                                  ALU.mult).then_inc(yd_used, 1)

            def sum_half(c, g, half):
                n = GROUPS * c + g
                dve.wait_ge(ya_used, NA * n + (NA if half else NA0))
                dve.wait_ge(yd_used, ND * n + (ND if half else ND0))
                if half:
                    dve.wait_ge(sums_done, 2 * n + 1)
                    wait_done(dve, g_done, n - GROUPS + 1)
                    src, out = prods[:, S_HALF:SLOTS, :], x2t[:, g, :]
                else:
                    src, out = prods[:, 0:S_HALF, :], prods[:, S_SUM, :]
                dve.tensor_reduce(out, src.rearrange("p s h -> p h s"), AX.X, ALU.add).then_inc(sums_done, 1)

            def split_x1(c, cols, high, done):
                dve.wait_ge(high, c + 1)
                dve.tensor_tensor(x1l[:, cols], x1[:, cols], x1h[:, cols].bitcast(F32),
                                  ALU.subtract).then_inc(done, 1)

            def sum_dims(c):
                dve.tensor_reduce(z[:, 0, bass.ds(c * CB, CB)].rearrange("p (g b) -> p g b", g=GROUPS),
                                  x1[:, :].rearrange("p (g d b) -> p g b d", g=GROUPS, d=D), AX.X,
                                  ALU.add).then_inc(z_sums, 1)

            def chunk(c, prev, nxt):
                for g in range(GROUPS):
                    for half in range(2):
                        own = [q for q in range(half * HALF, (half + 1) * HALF) if OWNERS[q] == "D"]
                        for q in own:
                            multiply(c, g, q)
                            if q != own[0]:
                                continue
                            if nxt and (g, half) == (GROUPS - 1, 1):
                                split_x1(c + 1, FRONT, x1h_front, x1_front)
                            if (g, half) == (0, 0):
                                split_x1(c, BACK, x1h_back, x1_back)
                            if half:
                                sum_half(c, g, 0)
                            elif g:
                                sum_half(c, g - 1, 1)
                            elif prev:
                                sum_half(c - 1, GROUPS - 1, 1)
                            if (g, half) == (1, 0):
                                sum_dims(c)

            dve.wait_ge(w0_in, 16)
            dve.tensor_tensor(w0[:, :, :].rearrange("p s h -> p (s h)"), w0ab[:, 0], w0ab[:, 1],
                              ALU.add).then_inc(w0_ready, 1)
            w1 = w2[:, :, :].rearrange("p j h -> p (j h)")
            for i in range(W1_PARTS):
                dve.wait_ge(w1h_ready, i + 1)
                dve.tensor_tensor(w1l[:, w1_part(i)], w1[:, w1_part(i)], w1h[:, w1_part(i)].bitcast(F32),
                                  ALU.subtract).then_inc(w1_split, 1)
            for i in range(T0):
                multiply0(dve, 0, i)
            dve.wait_ge(bias_in, 3 * 16)
            split_x1(0, FRONT, x1h_front, x1_front)
            chunk(0, False, True)
            with dve.Fori(1, CHUNKS - 1) as c:
                chunk(c, True, True)
            chunk(CHUNKS - 1, True, False)
            sum_half(CHUNKS - 1, GROUPS - 1, 1)

        @block.scalar
        def _(act):
            def evacuate_layout(c):
                act.wait_ge(lay_done, c + 1)
                wait_done(act, x0t_done, c)
                wait_done(act, scratch_in, 16 * c)
                act.activation(x0[:, :].rearrange("p (g d b) -> p g d b", g=GROUPS, d=D),
                               misc[0:FP, :].rearrange("p (d g b) -> p g d b", d=D, b=GB),
                               ACT.Copy).then_inc(x0_ready, 1)
                act.wait_ge(x0_ready, c + 1)
                act.dma_start(chunk_rows(c).rearrange("(u j) n -> j u n", u=COPIES),
                              x0[0:F, :].rearrange("p (u n) -> p u n", u=1).to_broadcast([F, COPIES, COLS]),
                              ).then_inc(scratch_in, 16)

            def evacuate_x0t(c):
                act.wait_ge(x0t_done, c + 1)
                act.activation(turned(c).rearrange("p (g j) -> p g j", j=F1)[:, :, 0:F],
                               misc[:, 0:GROUPS * F].rearrange("p (g j) -> p g j", j=F),
                               ACT.Copy).then_inc(x0t_ready, 1)

            def evacuate_x1(c):
                act.wait_ge(l0_done, T0 * (c + 1))
                wait_done(act, z_sums, c)
                act.activation(x1[:, :], acc0[:, :], ACT.Identity, bias=bias[:, 0:1]).then_inc(x1_ready, 1)
                act.wait_ge(x1_ready, c + 1)
                act.activation(x1h[:, FRONT], x1[:, FRONT], ACT.Copy).then_inc(x1h_front, 1)

            def split_back(c):
                wait_done(act, ya_ready, NA * GROUPS * c)
                act.activation(x1h[:, BACK], x1[:, BACK], ACT.Copy).then_inc(x1h_back, 1)

            def evacuate_gram(n):
                act.wait_ge(g_done, n + 1)
                act.activation(gram[:, :, bass.ds(n * GB, GB)],
                               misc[:, 0:GB * F1].rearrange("p (b j) -> p j b", b=GB),
                               ACT.Copy).then_inc(g_ready, 1)

            def multiply(c, g, q):
                n, k = GROUPS * c + g, OWNERS[:q].count("A")
                act.wait_ge(ya_ready, NA * n + k + 1)
                if k in (0, NA0):
                    wait_done(act, sums_done, 2 * n + (1 if k else 0) - 1)
                for i, j in enumerate(fields_of(q)):
                    mm = act.activation(prods[:, slot_of(q) + i, :], ya[(NA * g + k) % YA][:, i * H:(i + 1) * H], ACT.Copy,
                                        scale=turned(c)[:, g * F1 + j:g * F1 + j + 1])
                mm.then_inc(ya_used, 1)

            def chunk(c, prev, nxt, lay):
                split_back(c)
                for g in range(GROUPS):
                    for q in range(BLOCKS):
                        if OWNERS[q] == "A":
                            multiply(c, g, q)
                        if lay and (g, q) == (LAY_AFTER[0], LAY_AFTER[1] + 2):
                            evacuate_layout(c + 2)
                        if lay and (g, q) == (X0T_AFTER[0], X0T_AFTER[1] + 2):
                            evacuate_x0t(c + 2)
                        if q == G_AFTER + 1 and (g or prev):
                            evacuate_gram(GROUPS * c + g - 1)
                        if nxt and (g, q) == (L0_AFTER[-1][0], L0_AFTER[-1][1] - 1):
                            evacuate_x1(c + 1)

            act.wait_ge(bias_in, 3 * 16)
            act.mul(bias2d[:, :], bias[:, 1:2], float(D)).then_inc(bias2d_ready, 1)
            evacuate_layout(0)
            evacuate_x0t(0)
            act.wait_ge(w1_in, 16)
            w1 = w2[:, :, :].rearrange("p j h -> p (j h)")
            for i in range(W1_PARTS):
                act.activation(w1h[:, w1_part(i)], w1[:, w1_part(i)], ACT.Copy).then_inc(w1h_ready, 1)
            evacuate_x1(0)
            evacuate_layout(1)
            evacuate_x0t(1)
            chunk(0, False, True, True)
            with act.Fori(1, CHUNKS - 2) as c:
                chunk(c, True, True, True)
            chunk(CHUNKS - 2, True, True, False)
            chunk(CHUNKS - 1, True, False, False)
            evacuate_gram(GROUPS * CHUNKS - 1)
            act.wait_ge(tail_mm, 1)
            act.wait_ge(bias2d_ready, 1)
            act.activation(z[:, 1, :], yd[0][:, :], ACT.Identity, bias=bias2d[:, 0:1]).then_inc(tail_act, 1)
            act.wait_ge(mlp_in, 5 * 16)
            for m, src in enumerate(hid):
                act.wait_ge(tail_mm, 2 + m)
                act.activation(h1[:, m, :], src[:, :], ACT.Relu, bias=bt1[:, m:m + 1]).then_inc(tail_act, 1)
            for m, src in enumerate(hid2):
                act.wait_ge(tail_mm, 6 + m)
                act.activation(h2[:, m, :], src[:, :], ACT.Relu, bias=bt2[:, m:m + 1]).then_inc(tail_act, 1)
            act.wait_ge(tail_mm, 8)
            act.activation(y[:, :], yd[0][0:1, :], ACT.Copy).then_inc(tail_act, 1)


def constants():
    pack = np.zeros((P, C_ALL), np.float32)
    for row in range(P):
        pack[row, C_FI + row // CB] = 1.0
        pack[row, C_B + row % CB] = 1.0
        pack[row, C_MASK + row % GB] = 1.0
        pack[row, C_ID + row] = 1.0
    return pack


def layer0_layout(w):
    w = w.reshape(H, F, F)
    pair = np.zeros((K0, 2, T0, H), np.float32)
    i = np.arange(F)
    for tile in range(T0):
        for u in range(3):
            shift = 3 * tile + u
            if shift > F // 2:
                continue
            pair[R0 * u:R0 * u + F, 0, tile] = w[:, i, (i + shift) % F].T
            if shift:
                pair[R0 * u:R0 * u + F, 1, tile] = w[:, (i + shift) % F, i].T
    return pair.reshape(K0, 2, T0 * H)


def kernel(**inputs):
    import concourse.bacc as bacc
    from concourse.bass_utils import run_bass_kernel_spmd

    def host(name):
        return np.ascontiguousarray(np.asarray(inputs[name]))

    tables = [host(f"tbl_{f}") for f in range(F)]
    starts = np.cumsum([0] + [len(t) for t in tables])
    field = np.minimum(np.arange(FP), F - 1).reshape(FO, FI)
    arrays = {
        "tables": np.concatenate(tables),
        "ids": host("ids").reshape(CHUNKS, CB, F)[:, :, field].transpose(3, 1, 0, 2).reshape(P, CHUNKS, FO),
        "first_row": np.repeat(starts[field.T].astype(np.int32), CB, axis=0),
        "const": constants(),
        "w0ab": layer0_layout(host("L0_rec_W0")),
        "w1": host("L0_rec_W1").reshape(H, F, H).transpose(2, 1, 0),
        "w2": host("L0_rec_W2").reshape(H, F, H).transpose(2, 1, 0),
        "b0": host("L0_rec_b0"), "b1": host("L0_rec_b1"), "b2": host("L0_rec_b2"),
        "W_top1": host("W_top1"), "W_top2": host("W_top2"),
        "dense_t": host("dense_ctx").T,
        "w_top3": host("W_top3").reshape(HID2 // P, P).T,
        "b_top1": host("b_top1").reshape(HID1 // P, P).T,
        "b_top2": host("b_top2").reshape(HID2 // P, P).T,
    }
    nc = bacc.Bacc("TRN2", target_bir_lowering=False, num_devices=1)
    aps = {}
    for name in arrays:
        arrays[name] = np.ascontiguousarray(arrays[name])
        aps[name] = nc.dram_tensor(f"in_{name}", arrays[name].shape, mybir.dt.from_np(arrays[name].dtype),
                                   kind="ExternalInput").ap()
    aps["out"] = nc.dram_tensor("out_y", (B, 1), F32, kind="ExternalOutput").ap()
    build(nc, aps)
    r = run_bass_kernel_spmd(nc, [{f"in_{n}": v for n, v in arrays.items()}], core_ids=[0])
    return r.results[0]["out_y"]
```
